# Optimizing a Trainium2 kernel written in Bass

```python
import numpy as np
import jax
import jax.numpy as jnp

def _softmax(x, axis=-1):
    return jax.nn.softmax(x, axis=axis)

def _gelu(x):
    return jax.nn.gelu(x, approximate=True)

def _silu(x):
    return jax.nn.silu(x)

def _sigmoid(x):
    return jax.nn.sigmoid(x)

def _layernorm(x, axis=-1, eps=1e-05):
    m = jnp.mean(x, axis=axis, keepdims=True)
    v = jnp.var(x, axis=axis, keepdims=True)
    return (x - m) / jnp.sqrt(v + eps)

def _scatter_add(tgt, idx, src, axis=0):
    return tgt.at[idx].add(src)

def _segment_sum(src, seg, n):
    return jax.ops.segment_sum(src, seg, n)
kernel_name = 'mk_xattn_ffn_d1_seqx_r4_7d4b97'

def setup_inputs(seed: int=0):
    np.random.seed(seed)
    _w = jnp.asarray

    def _rec_inputs():
        import jax
        import jax.numpy as jnp
        _rk = jax.random.key(seed)
        x = -0.0002928 + 1 * jax.random.normal(jax.random.fold_in(_rk, 1), (4, 1024, 256), jnp.float32)
        _lenS = 1024 - jax.random.randint(jax.random.fold_in(_rk, 7), (4,), 0, max(1, 1024 // 4) + 1, jnp.int32)
        _lenS2 = 77 - jax.random.randint(jax.random.fold_in(_rk, 8), (4,), 0, max(1, 77 // 4) + 1, jnp.int32)
        _ctx_1024P = jax.random.normal(jax.random.fold_in(_rk, 11), (4, 16, 256), jnp.float32)
        _ctx_1024c = jax.random.dirichlet(jax.random.fold_in(_rk, 511), 0.3 * jnp.ones((16,), jnp.float32), (4, 77))
        _ctx_1024t = jnp.einsum('bsk,bkd->bsd', _ctx_1024c, _ctx_1024P)
        _ctx_1024t = _ctx_1024t * jax.lax.rsqrt(jnp.mean(jnp.square(_ctx_1024t)) + 1e-12) * 0.953939
        ctx_1024 = -1.39393e-06 + 0.999914 * (_ctx_1024t + 0.3 * jax.random.normal(jax.random.fold_in(_rk, 611), (4, 77, 256), jnp.float32))
        _validS = jnp.arange(1024)[None, :] < _lenS[:, None]
        _validS2 = jnp.arange(77)[None, :] < _lenS2[:, None]
        _causal = jnp.tril(jnp.ones((1024, 1024), dtype=bool))
        mask_BxS2_bk0 = jnp.logical_not(jnp.broadcast_to(_validS2[:, :], (4, 77)))
        return (x, ctx_1024, mask_BxS2_bk0)
    x, ctx_1024, mask_BxS2_bk0 = _rec_inputs()

    def _L0_xattn_setup():
        import jax, jax.numpy as jnp
        import numpy as np
        EMBED_DIM = 256
        NUM_HEADS = 16
        HEAD_DIM = EMBED_DIM // NUM_HEADS
        key = jax.random.key(seed)
        ks = jax.random.split(key, 12)
        B, S, E = (2, 512, EMBED_DIM)
        scale = 1.0 / np.sqrt(E)
        inp = {'query': jax.random.normal(ks[0], (B, S, E), dtype=jnp.float32), 'key': jax.random.normal(ks[1], (B, S, E), dtype=jnp.float32), 'value': jax.random.normal(ks[2], (B, S, E), dtype=jnp.float32), 'key_padding_mask': jax.random.randint(ks[3], (B, S), 0, 2).astype(bool), 'Wq': jax.random.normal(ks[4], (E, E), dtype=jnp.float32) * scale, 'bq': jnp.zeros((E,), dtype=jnp.float32), 'Wk': jax.random.normal(ks[5], (E, E), dtype=jnp.float32) * scale, 'bk': jnp.zeros((E,), dtype=jnp.float32), 'Wv': jax.random.normal(ks[6], (E, E), dtype=jnp.float32) * scale, 'bv': jnp.zeros((E,), dtype=jnp.float32), 'Wo': jax.random.normal(ks[7], (E, E), dtype=jnp.float32) * scale, 'bo': jnp.zeros((E,), dtype=jnp.float32)}
        return inp
    _L0_xattn_all = _L0_xattn_setup()
    _L0_xattn_in = {k: v for k, v in _L0_xattn_all.items() if k in ('Wq', 'bq', 'Wk', 'bk', 'Wv', 'bv', 'Wo', 'bo')}
    del _L0_xattn_all

    def _L0_ffn_setup():
        import jax, jax.numpy as jnp
        import numpy as np
        N_EXPERTS = 8
        CAP_FACTOR = 1.25
        BATCH, SEQ, DMODEL, DFF = (4, 512, 256, 1024)
        key = jax.random.key(seed)
        k0, k1, k2, k3 = jax.random.split(key, 4)
        x = jax.random.normal(k0, (BATCH, SEQ, DMODEL), dtype=jnp.float32)
        Wr = jax.random.normal(k1, (DMODEL, N_EXPERTS), dtype=jnp.float32) * 0.02
        W1 = jax.random.normal(k2, (N_EXPERTS, DMODEL, DFF), dtype=jnp.float32) * 0.02
        W2 = jax.random.normal(k3, (N_EXPERTS, DFF, DMODEL), dtype=jnp.float32) * 0.02
        return {'x': x, 'Wr': Wr, 'W1': W1, 'W2': W2}
    _L0_ffn_all = _L0_ffn_setup()
    _L0_ffn_in = {k: v for k, v in _L0_ffn_all.items() if k in ('Wr', 'W1', 'W2')}
    del _L0_ffn_all
    return {'x': x, 'ctx_1024': ctx_1024, 'mask_BxS2_bk0': mask_BxS2_bk0, 'L0_xattn_Wq': _L0_xattn_in['Wq'], 'L0_xattn_bq': _L0_xattn_in['bq'], 'L0_xattn_Wk': _L0_xattn_in['Wk'], 'L0_xattn_bk': _L0_xattn_in['bk'], 'L0_xattn_Wv': _L0_xattn_in['Wv'], 'L0_xattn_bv': _L0_xattn_in['bv'], 'L0_xattn_Wo': _L0_xattn_in['Wo'], 'L0_xattn_bo': _L0_xattn_in['bo'], 'L0_ffn_Wr': _L0_ffn_in['Wr'], 'L0_ffn_W1': _L0_ffn_in['W1'], 'L0_ffn_W2': _L0_ffn_in['W2']}

def reference(x, ctx_1024, mask_BxS2_bk0, L0_xattn_Wq, L0_xattn_bq, L0_xattn_Wk, L0_xattn_bk, L0_xattn_Wv, L0_xattn_bv, L0_xattn_Wo, L0_xattn_bo, L0_ffn_Wr, L0_ffn_W1, L0_ffn_W2):
    import jax
    import jax.numpy as jnp

    def _L0_xattn_ref(query, key, value, key_padding_mask, Wq, bq, Wk, bk, Wv, bv, Wo, bo):
        import jax, jax.numpy as jnp
        import numpy as np
        EMBED_DIM = 256
        NUM_HEADS = 16
        HEAD_DIM = EMBED_DIM // NUM_HEADS
        B, Sq, E = query.shape
        H, D = (NUM_HEADS, HEAD_DIM)

        def split_heads(x, W, b):
            y = x @ W.T + b
            return y.reshape(B, -1, H, D).transpose(0, 2, 1, 3)
        q = split_heads(query, Wq, bq)
        k = split_heads(key, Wk, bk)
        v = split_heads(value, Wv, bv)
        scores = jnp.einsum('bhqd,bhkd->bhqk', q, k) / jnp.sqrt(jnp.float32(D))
        scores = jnp.where(key_padding_mask[:, None, None, :], -jnp.inf, scores)
        probs = jax.nn.softmax(scores, axis=-1)
        attn = jnp.einsum('bhqk,bhkd->bhqd', probs, v)
        attn = attn.transpose(0, 2, 1, 3).reshape(B, Sq, E)
        return attn @ Wo.T + bo

    def _L0_ffn_ref(x, Wr, W1, W2):
        import jax, jax.numpy as jnp
        import numpy as np
        N_EXPERTS = 8
        CAP_FACTOR = 1.25
        BATCH, SEQ, DMODEL, DFF = (4, 512, 256, 1024)
        B, S, D = x.shape
        E = W1.shape[0]
        cap = int(CAP_FACTOR * B * S / E)
        t = x.reshape(-1, D)
        probs = jax.nn.softmax(t @ Wr, axis=-1)
        idx = jnp.argmax(probs, axis=-1)
        pmax = jnp.max(probs, axis=-1)
        onehot = jax.nn.one_hot(idx, E, dtype=jnp.int32)
        pos = jnp.sum(jnp.cumsum(onehot, axis=0) * onehot, axis=-1) - 1
        kept = pos < cap
        flat = idx * cap + jnp.minimum(pos, cap - 1)
        disp = jnp.zeros((E * cap, D), t.dtype).at[flat].add(t * kept[:, None].astype(t.dtype))
        ein = disp.reshape(E, cap, D)
        h = jax.nn.relu(jnp.einsum('ecd,edf->ecf', ein, W1))
        eout = jnp.einsum('ecf,efd->ecd', h, W2).reshape(E * cap, D)
        comb = jnp.where(kept[:, None], eout[flat], t)
        factor = jnp.where(kept, pmax, jnp.ones_like(pmax))
        out = (comb * factor[:, None]).reshape(B, S, D)
        return out
    x = x + _L0_xattn_ref(_layernorm(x, axis=-1), ctx_1024, ctx_1024, mask_BxS2_bk0, L0_xattn_Wq, L0_xattn_bq, L0_xattn_Wk, L0_xattn_bk, L0_xattn_Wv, L0_xattn_bv, L0_xattn_Wo, L0_xattn_bo)
    x = x + _L0_ffn_ref(_layernorm(x, axis=-1), L0_ffn_Wr, L0_ffn_W1, L0_ffn_W2)
    return x

_drawn_inputs = setup_inputs


def setup_inputs(seed=0):
    import zlib

    import numpy as np

    out = dict(_drawn_inputs(seed))
    spreads = {'L0_xattn_bq': (0.0, 0.1),
     'L0_xattn_bk': (0.0, 0.8),
     'L0_xattn_bv': (0.0, 0.1),
     'L0_xattn_bo': (0.0, 0.1)}
    factors = {'L0_ffn_W1': 3.456, 'L0_ffn_W2': 2.847}
    for name, (base, spread) in spreads.items():
        noise = np.random.default_rng([zlib.crc32(name.encode()), seed]).standard_normal(out[name].shape)
        drawn = base * np.exp(spread * noise) if base else spread * noise
        out[name] = jnp.asarray(drawn.astype(out[name].dtype))
    for name, factor in factors.items():
        out[name] = (out[name] * factor).astype(out[name].dtype)
    return out
```

```python
from contextlib import ExitStack

import numpy as np

import concourse.bass as bass
from concourse import mybir
from concourse.alu_op_type import AluOpType as ALU

F32 = mybir.dt.float32
BF16 = mybir.dt.bfloat16
I32 = mybir.dt.int32
U8 = mybir.dt.uint8
ACT = mybir.ActivationFunctionType
AX = mybir.AxisListType

P = 128
B, S, D = 4, 1024, 256
H = 16
DH = D // H
SK = 77
E, FF = 8, 1024
TOK = B * S
CAP = int(1.25 * TOK / E)
KD = D // P
HH = H // KD
HQ = HH // 2
TPG = 4
GT = TPG * P
NG = TOK // GT
GPB = S // GT
CH = -(-HH * SK // P)
PAD = (CH * P - HH * SK)
FC = FF // P
SC = CAP // P
CW = CAP // 2
ROW = D + 4
MEAN, RSTD, GATE, TOKEN = D, D + 1, D + 2, D + 3
EPS = 1e-5
MASKED = -3.0e38
FAR = 65536.0
GPI = 2


def wait(eng, sem, value):
    if isinstance(value, int) and value <= 0:
        return
    eng.wait_ge(sem, value)


class Stage:

    def __init__(self, pair, parity):
        self.pair, self.parity = pair, parity

    def count(self, per, more=0):
        if isinstance(self.pair, int):
            return per * (GPI * self.pair + self.parity) + more
        return self.pair * (GPI * per) + (per * self.parity + more)

    def turns(self, per, more=0):
        return self.pair * per + more


def pipeline(eng, step):

    def at(g):
        return Stage(g // GPI, g % GPI) if 0 <= g < NG else None

    def peeled(g):
        step(at(g + 1), at(g), at(g - 1), at(g - 2))

    for g in range(-1, GPI):
        peeled(g)
    with eng.Fori(1, NG // GPI - 1) as pair:
        for par in range(GPI):
            stages = []
            for lag in (-1, 0, 1, 2):
                q = (par - lag) % GPI
                stages.append(Stage(pair + (par - lag - q) // GPI, q))
            step(*stages)
    for g in range(NG - GPI, NG + 2):
        peeled(g)


def experts(eng, step):
    step(Stage(0, 0), Stage(0, 1))
    step(Stage(0, 1), Stage(1, 0))
    with eng.Fori(1, E // GPI - 1) as pair:
        step(Stage(pair, 0), Stage(pair, 1))
        step(Stage(pair, 1), Stage(pair + 1, 0))
    step(Stage(E // GPI - 1, 0), Stage(E // GPI - 1, 1))
    step(Stage(E // GPI - 1, 1), None)


def xattn_moe(nc, x, ctxT, mask, wqT, bq, wkT, bk, wvT, bv, woT, bo, wr, w1, w2, out):
    ctx = ExitStack()
    with ctx:
        def sb(name, shape, dt=F32):
            return ctx.enter_context(nc.sbuf_tensor(name, shape, dt))

        def sem(name):
            return ctx.enter_context(nc.semaphore(name))

        slots_dram = nc.dram_tensor("slot_rows", (E * CAP, ROW), F32, kind="Internal").ap()

        ident = sb("ident", [P, P])
        before = sb("before", [P, P], BF16)
        ones = sb("ones", [P, P], BF16)
        headmask = sb("headmask", [P, HH])
        zeros = sb("zeros", [P, ROW])
        token_no = sb("token_no", [P, TOK // P])
        rank = sb("rank", [P, TPG, E])
        neg_half = sb("neg_half", [P, TPG])
        wq_sb = sb("wq_sb", [P, KD, D])
        wk_sb = sb("wk_sb", [P, KD, D])
        wv_sb = sb("wv_sb", [P, KD, D])
        wo_sb = sb("wo_sb", [P, KD, D])
        wr_sb = sb("wr_sb", [P, KD, P])
        bq_sb = sb("bq_sb", [P, KD])
        bk_sb = sb("bk_sb", [P, KD])
        bv_sb = sb("bv_sb", [P, D])
        bo_sb = sb("bo_sb", [P, D])
        ctx_sb = sb("ctx_sb", [P, KD, B * SK])
        mask_u8 = sb("mask_u8", [1, B * SK], U8)
        mask_row = sb("mask_row", [P, B, HQ * SK], BF16)

        x_sb = sb("x_sb", [P, TOK // P, D])
        kT = sb("kT", [P, KD, B * SK])
        kblk_mem = sb("kblk_mem", [P, B * KD * HH * SK])
        v_nat = sb("v_nat", [SK, B, D])
        vblk_mem = sb("vblk_mem", [P, B * KD * CH * P])
        v_now = sb("v_now", [P, KD * CH, P])
        xn = sb("xn", [P, TPG, D])
        xnT = sb("xnT", [P, KD, GT])
        qT = [sb(f"qT{i}", [P, KD, GT]) for i in range(GPI)]
        probs = [sb(f"probs{i}", [P, H * SK + PAD]) for i in range(2)]
        rowmax = sb("rowmax", [P, 2, H])
        sums = sb("sums", [P, TPG, H])
        rsum = sb("rsum", [P, TPG, H])
        rsum_wide = sb("rsum_wide", [P, TPG, D])
        probsT_mem = [sb(f"probsT{i}", [P, KD * CH * GT]) for i in range(GPI)]
        attnU = sb("attnU", [P, KD, GT])
        attnT = sb("attnT", [P, KD, GT])
        rows = [sb(f"rows{i}", [P, TPG, ROW]) for i in range(GPI)]
        t_sb = sb("t_sb", [P, TPG, D])
        tT = sb("tT", [P, KD, GT])
        base = sb("base", [P, TPG, D])
        bn1 = sb("bn1", [P, TPG, 6])
        mv1 = sb("mv1", [P, TPG, 2])
        bn2 = sb("bn2", [P, TPG, 6])
        mv2 = sb("mv2", [P, TPG, 2])
        var1, y1, yy1, rstd1 = (sb(f"ln1_{i}", [P, TPG]) for i in range(4))
        var2, y2, yy2, rstd2 = (sb(f"ln2_{i}", [P, TPG]) for i in range(4))

        lgT = sb("lgT", [P, GT])
        lmax = sb("lmax", [P, TPG])
        lsh = sb("lsh", [P, TPG, E])
        lexp = sb("lexp", [P, TPG, E])
        cand = sb("cand", [P, TPG, E])
        cmax = sb("cmax", [P, TPG])
        onehot = sb("onehot", [P, TPG, E], BF16)
        taken = sb("taken", [P, E], BF16)
        group_taken = sb("group_taken", [P, E])
        posm = sb("posm", [P, TPG, E])
        pos = sb("pos", [P, TPG])
        keep = sb("keep", [P, TPG])
        esum = sb("esum", [P, TPG])
        pmax = sb("pmax", [P, TPG])
        past = sb("past", [P, TPG])
        first = sb("first", [P, TPG])
        slotf = sb("slotf", [P, TPG])
        slot = [sb(f"slot{i}", [P, TPG], I32) for i in range(GPI)]
        drop, drs, scale_b, shift_b = (sb(f"base_{i}", [P, TPG]) for i in range(4))

        kblk = kblk_mem[:, :].rearrange("p (b m h k) -> p b m h k", b=B, m=KD, h=HH)
        kflat = kblk_mem[:, :].rearrange("p (b m c) -> p b m c", b=B, m=KD)
        vblk = vblk_mem[:, :].rearrange("p (b c n) -> p b c n", b=B, c=KD * CH)
        probsT = [t[:, :].rearrange("p (c n) -> p c n", c=KD * CH) for t in probsT_mem]
        w_mem = [vblk_mem, kblk_mem]
        w1_sb = [m[:, 0:KD * FF].rearrange("p (k f) -> p k f", k=KD) for m in w_mem]
        w2_sb = [m[:, KD * FF:KD * FF + FC * D].rearrange("p (c d) -> p c d", c=FC) for m in w_mem]
        hidden = probsT_mem[0][:, 0:FC * CAP].rearrange("p (c s) -> p c s", c=FC)
        spare = probsT_mem[1]
        t_slots = spare[:, 0:SC * D].rearrange("p (s d) -> p s d", s=SC)
        tT_slots = spare[:, SC * D:2 * SC * D].rearrange("p (k s) -> p k s", k=KD)
        y_sb = [spare[:, (2 + i) * SC * D:(3 + i) * SC * D].rearrange("p (s d) -> p s d", s=SC) for i in range(GPI)]
        x_flat = x_sb[:, :, :].rearrange("p t d -> p (t d)")
        srow = [x_flat[:, i * SC * ROW:(i + 1) * SC * ROW].rearrange("p (s r) -> p s r", s=SC) for i in range(GPI)]
        empty = sb("empty", [P, SC])
        dest = [sb(f"dest{i}", [P, SC], I32) for i in range(GPI)]

        sc_ps = ctx.enter_context(nc.psum_tensor("sc_ps", [P, 4, 512], F32))
        pt = [ctx.enter_context(nc.psum_tensor(f"pt{i}", [P, 512], F32)) for i in range(2)]
        wk = [ctx.enter_context(nc.psum_tensor(f"wk{i}", [P, 512], F32)) for i in range(2)]
        scores = sc_ps[:, :, 0:HQ * SK].rearrange("p q (h k) -> p q h k", h=HQ)

        kv_loaded = sem("kv_loaded")
        w_attn_loaded = sem("w_attn_loaded")
        x_loaded = [sem(f"x_loaded{i}") for i in range(GPI)]
        v_placed = sem("v_placed")
        slots_zeroed = sem("slots_zeroed")
        rows_free = sem("rows_free")
        rows_sent = [sem(f"rows_sent{i}") for i in range(GPI)]
        base_stored = sem("base_stored")
        w_loaded = [sem(f"w_loaded{i}") for i in range(GPI)]
        srow_loaded = [sem(f"srow_loaded{i}") for i in range(GPI)]
        y_sent = [sem(f"y_sent{i}") for i in range(GPI)]
        consts_set = sem("consts_set")
        consts_cut = sem("consts_cut")
        mask_ready = sem("mask_ready")
        kT_ps = sem("kT_ps")
        kT_ready = sem("kT_ready")
        kblk_ready = sem("kblk_ready")
        v_ps = sem("v_ps")
        v_nat_ready = sem("v_nat_ready")
        vblk_zeroed = sem("vblk_zeroed")
        v_now_ready = sem("v_now_ready")
        bn1_done = sem("bn1_done")
        moments1 = sem("moments1")
        rstd1_step = sem("rstd1_step")
        rstd1_ready = sem("rstd1_ready")
        xn_ready = sem("xn_ready")
        xb_ready = sem("xb_ready")
        xnT_ps = sem("xnT_ps")
        xnT_ready = sem("xnT_ready")
        q_ps = sem("q_ps")
        q_ready = sem("q_ready")
        scores_ready = sem("scores_ready")
        rowmax_ready = sem("rowmax_ready")
        shifted = sem("shifted")
        probs_ready = sem("probs_ready")
        sums_ready = sem("sums_ready")
        rsum_ready = sem("rsum_ready")
        probsT_ps = sem("probsT_ps")
        probsT_ready = sem("probsT_ready")
        rsum_wide_ready = sem("rsum_wide_ready")
        rsumT_ps = sem("rsumT_ps")
        attn_ps = sem("attn_ps")
        attnU_ready = sem("attnU_ready")
        attnT_ready = sem("attnT_ready")
        proj_ps = sem("proj_ps")
        x1_ready = sem("x1_ready")
        bn2_done = sem("bn2_done")
        moments2 = sem("moments2")
        rstd2_step = sem("rstd2_step")
        t_ready = sem("t_ready")
        tT_ps = sem("tT_ps")
        tT_ready = sem("tT_ready")
        lgT_ps = sem("lgT_ps")
        lgT_ready = sem("lgT_ready")
        logits_ps = sem("logits_ps")
        choice_step = sem("choice_step")
        lsh_ready = sem("lsh_ready")
        lexp_ready = sem("lexp_ready")
        onehot_ready = sem("onehot_ready")
        taken_ready = sem("taken_ready")
        prefix_ps = sem("prefix_ps")
        posm_ready = sem("posm_ready")
        place_step = sem("place_step")
        route_ready = sem("route_ready")
        base_step = sem("base_step")
        base_ready = sem("base_ready")
        t_slots_ready = sem("t_slots_ready")
        empty_ready = sem("empty_ready")
        dest_ready = sem("dest_ready")
        tT_slots_ps = sem("tT_slots_ps")
        tT_slots_ready = sem("tT_slots_ready")
        hidden_ps = sem("hidden_ps")
        hidden_ready = [sem(f"hidden_ready{i}") for i in range(2)]
        y_ps = sem("y_ps")
        y_ready = sem("y_ready")

        x_tiles = x.rearrange("b s d -> (b s) d").rearrange("(t p) d -> p t d", p=P)
        out_rows = out.rearrange("b s d -> (b s) d")
        out_tiles = out_rows.rearrange("(t p) d -> p t d", p=P)
        V_PARTS = KD * (HH + sum(1 for h in range(HH) if h * SK // P != ((h + 1) * SK - 1) // P))
        ATTN_W_LOADS = 5
        KV_LOADS = 6

        def group(s, j=0, n=TPG):
            if isinstance(s.pair, int):
                t = TPG * (GPI * s.pair + s.parity) + j
                return slice(t, t + n)
            return bass.ds(s.pair * (GPI * TPG) + (TPG * s.parity + j), n)

        block = ctx.enter_context(nc.Block())

        waits_passed = sem("waits_passed")

        def wait_alone(eng, sem, value):
            wait(eng, sem, value)
            if not isinstance(value, int):
                eng.sem_inc(waits_passed, 1)

        @block.sync
        def _(sp):
            def load_x(s):
                wait(sp, x_loaded[s.parity], s.turns(16))
                sp.dma_start(x_sb[:, group(s), :], x_tiles[:, group(s), :]).then_inc(x_loaded[s.parity], 16)

            sp.sem_inc(base_stored, 16)
            load_x(Stage(0, 0))
            sp.dma_start(wq_sb[:, :, :], wqT.rearrange("(k p) n -> p k n", p=P)).then_inc(w_attn_loaded, 16)
            sp.dma_start(bq_sb[:, :], bq[:, :]).then_inc(w_attn_loaded, 16)
            load_x(Stage(0, 1))
            sp.dma_start(wo_sb[:, :, :], woT.rearrange("(k p) n -> p k n", p=P)).then_inc(w_attn_loaded, 16)
            sp.dma_start(bo_sb[:, :], bo.rearrange("(a n) -> a n", a=1).broadcast_to([P, D])).then_inc(w_attn_loaded, 16)
            sp.wait_ge(consts_set, 1)
            sp.dma_start(wr_sb[:, :, 0:E], wr.rearrange("(k p) e -> p k e", p=P)).then_inc(w_attn_loaded, 16)
            with sp.Fori(1, NG // GPI) as pair:
                for par in range(GPI):
                    load_x(Stage(pair, par))
            sp.wait_ge(v_nat_ready, B // 2)
            sp.wait_ge(vblk_zeroed, 1)
            for h in range(HH):
                r = h * SK
                while r < (h + 1) * SK:
                    end = min((h + 1) * SK, (r // P + 1) * P)
                    for m in range(KD):
                        c, k0 = m * CH + r // P, r - h * SK
                        cols = (m * HH + h) * DH
                        sp.dma_start(vblk[r % P:r % P + end - r, :, c, h * DH:(h + 1) * DH],
                                     v_nat[k0:k0 + end - r, :, cols:cols + DH]).then_inc(v_placed, 16)
                    r = end
            sp.wait_ge(consts_set, 1)
            sp.dma_start(slots_dram.rearrange("(p s) r -> p s r", p=P),
                         zeros[:, None, :].broadcast_to([P, E * CAP // P, ROW])).then_inc(slots_zeroed, 16)

            def load_weights(e, number):
                sp.dma_start(w1_sb[e.parity], w1[number].rearrange("e (k p) f -> p (e k) f", p=P)).then_inc(w_loaded[e.parity], 16)
                sp.dma_start(w2_sb[e.parity], w2[number].rearrange("e (c p) d -> p (e c) d", p=P)).then_inc(w_loaded[e.parity], 16)

            def step(nxt, cur, prev, old):
                if old:
                    wait(sp, base_ready, old.count(1, 2))
                    sp.dma_start(out_tiles[:, group(old), :], base[:, :, :]).then_inc(base_stored, 16)

            pipeline(sp, step)
            sp.wait_ge(v_now_ready, B)
            load_weights(Stage(0, 0), slice(0, 1))
            sp.wait_ge(scores_ready, TOK // P)
            load_weights(Stage(0, 1), slice(1, 2))

            def load_slots(e):
                if isinstance(e.pair, int):
                    n = (GPI * e.pair + e.parity) * CAP
                    src = slots_dram[n:n + CAP, :]
                else:
                    src = slots_dram[bass.ds(e.pair * (GPI * CAP) + e.parity * CAP, CAP), :]
                wait(sp, y_ready, e.count(SC, -SC))
                sp.dma_start(srow[e.parity], src.rearrange("(s p) r -> p s r", p=P)).then_inc(srow_loaded[e.parity], 16)

            for par in range(GPI):
                sp.wait_ge(rows_sent[par], 16 * TOK // P // GPI)
            for par in range(GPI):
                load_slots(Stage(0, par))
            with sp.Fori(1, E // GPI) as pair:
                for par in range(GPI):
                    e = Stage(pair, par)
                    load_slots(e)
                    wait(sp, y_ps, e.count(SC, -SC))
                    load_weights(e, bass.ds(pair * GPI + par, 1))
            sp.wait_ge(base_stored, 16 * (NG + 1))

        @block.gpsimd
        def _(pool):
            pool.sem_inc(rows_free, GPI)
            pool.sem_inc(base_ready, 1)
            pool.memset(zeros[:, :], 0.0)
            pool.memset(wr_sb[:, :, :], 0.0).then_inc(consts_set, 1)
            pool.memset(ident[:, :], 1.0)
            pool.memset(before[:, :], 1.0)
            pool.memset(ones[:, :], 1.0)
            pool.memset(headmask[:, :], 1.0)
            pool.memset(taken[:, :], 0.0).then_inc(taken_ready, 1)
            pool.memset(neg_half[:, :], -0.5)
            for q in probs:
                pool.memset(q[:, H * SK:], 0.0)
            pool.memset(mask_row[:, :, :], 0.0).then_inc(consts_set, 1)
            pool.wait_ge(consts_set, 2)
            pool.affine_select(out=ident[:, :], in_=ident[:, :], compare_op=ALU.is_equal, fill=0.0,
                               base=0, pattern=[[-1, P]], channel_multiplier=1)
            pool.affine_select(out=before[:, :], in_=before[:, :], compare_op=ALU.is_gt, fill=0.0,
                               base=0, pattern=[[1, P]], channel_multiplier=-1)
            pool.iota(token_no[:, :], [[P, TOK // P]], base=1, channel_multiplier=1,
                      allow_small_or_imprecise_dtypes=True)
            pool.iota(rank[:, :, :], [[0, TPG], [-1, E]], base=E, channel_multiplier=0,
                      allow_small_or_imprecise_dtypes=True)
            pool.affine_select(out=headmask[:, :], in_=headmask[:, :], compare_op=ALU.is_ge, fill=0.0,
                               base=0, pattern=[[-DH, HH]], channel_multiplier=1).then_inc(consts_cut, 1)
            pool.wait_ge(consts_cut, 1)
            pool.affine_select(out=headmask[:, :], in_=headmask[:, :], compare_op=ALU.is_ge, fill=0.0,
                               base=DH - 1, pattern=[[DH, HH]], channel_multiplier=-1).then_inc(consts_cut, 1)

            def inverse_std(s, var, moments, y, yy, result, step, steps, mv):
                def then(k, ins):
                    ins.then_inc(step, 1)
                    (wait_alone if k == 4 else wait)(pool, step, s.count(steps, k))
                wait_alone(pool, moments, s.count(1, 1))
                then(1, pool.tensor_scalar(var[:, :], mv[:, :, 1], EPS, None, ALU.add))
                then(2, pool.tensor_tensor(y[:, :], var[:, :], neg_half[:, :], ALU.pow))
                then(3, pool.tensor_tensor(yy[:, :], y[:, :], y[:, :], ALU.mult))
                then(4, pool.tensor_tensor(yy[:, :], yy[:, :], var[:, :], ALU.mult))
                then(5, pool.tensor_scalar(yy[:, :], yy[:, :], -0.5, 1.5, ALU.mult, ALU.add))
                return pool.tensor_tensor(result, y[:, :], yy[:, :], ALU.mult)

            def rstd_first(s):
                wait(pool, xn_ready, s.count(1))
                inverse_std(s, var1, moments1, y1, yy1, rstd1[:, :], rstd1_step, 5, mv1).then_inc(rstd1_ready, 1)

            def spread_rsum(s):
                wait(pool, rsum_ready, s.count(1, 1))
                wait_alone(pool, rsumT_ps, s.count(KD))
                pool.tensor_copy(rsum_wide[:, :, :].rearrange("p t (h d) -> p t h d", h=H),
                                 rsum[:, :, :, None].broadcast_to([P, TPG, H, DH])).then_inc(rsum_wide_ready, 1)

            def add_output_bias(s):
                wait(pool, xn_ready, s.count(1, 1))
                pool.tensor_tensor(x_sb[:, group(s), :], x_sb[:, group(s), :],
                                   bo_sb[:, None, :].broadcast_to([P, TPG, D]), ALU.add).then_inc(xb_ready, 1)

            def second_norm(s):
                r = rows[s.parity]
                inverse_std(s, var2, moments2, y2, yy2, rstd2[:, :], rstd2_step, 8, mv2).then_inc(rstd2_step, 1)
                wait_alone(pool, rstd2_step, s.count(8, 6))
                pool.tensor_copy(r[:, :, RSTD], rstd2[:, :]).then_inc(rstd2_step, 1)
                pool.tensor_copy(r[:, :, MEAN], mv2[:, :, 0]).then_inc(rstd2_step, 1)
                pool.wait_ge(rstd2_step, s.count(8, 8))
                wait_alone(pool, tT_ps, s.count(KD))
                for j in range(TPG):
                    last = pool.tensor_scalar(t_sb[:, j, :], r[:, j, 0:D], r[:, j, MEAN:MEAN + 1], r[:, j, RSTD:RSTD + 1],
                                              ALU.subtract, ALU.mult)
                last.then_inc(t_ready, 1)

            def rows_without_expert(s):
                r = rows[s.parity]
                wait_alone(pool, base_stored, s.count(16, 16))
                pool.tensor_scalar(drop[:, :], keep[:, :], -1.0, 1.0, ALU.mult, ALU.add).then_inc(base_step, 1)
                pool.wait_ge(base_step, s.count(3, 1))
                pool.tensor_tensor(drs[:, :], drop[:, :], r[:, :, RSTD], ALU.mult).then_inc(base_step, 1)
                wait_alone(pool, base_step, s.count(3, 2))
                pool.tensor_scalar(scale_b[:, :], drs[:, :], 1.0, None, ALU.add)
                pool.tensor_tensor(shift_b[:, :], drs[:, :], r[:, :, MEAN], ALU.mult).then_inc(base_step, 1)
                wait_alone(pool, base_step, s.count(3, 3))
                for j in range(TPG):
                    last = pool.tensor_scalar(base[:, j, :], r[:, j, 0:D], scale_b[:, j:j + 1], shift_b[:, j:j + 1],
                                              ALU.mult, ALU.subtract)
                last.then_inc(base_ready, 1)

            def dispatch(s):
                wait_alone(pool, route_ready, s.count(1, 1))
                for j in range(TPG):
                    pool.indirect_dma_start(slots_dram, bass.IndirectOffsetOnAxis(ap=slot[s.parity][:, j:j + 1], axis=0),
                                            rows[s.parity][:, j, :], None, bounds_check=E * CAP - 1,
                                            oob_is_err=False).then_inc(rows_sent[s.parity], 16)

            def step(nxt, cur, prev, old):
                if prev and old is None:
                    pool.wait_ge(slots_zeroed, 16)
                if prev:
                    spread_rsum(prev)
                if nxt:
                    rstd_first(nxt)
                if cur is None and nxt:
                    for b in range(B):
                        for m in range(KD):
                            if b == 0 and m == 0:
                                pool.wait_ge(kT_ready, KD)
                            pool.tensor_tensor(
                                kblk[:, b, m, :, :],
                                kT[:, m, b * SK:(b + 1) * SK][:, None, :].broadcast_to([P, HH, SK]),
                                headmask[:, :][:, :, None].broadcast_to([P, HH, SK]), ALU.mult).then_inc(kblk_ready, 1)
                    pool.memset(vblk_mem[:, :], 0.0).then_inc(vblk_zeroed, 1)
                    pool.wait_ge(w_attn_loaded, 16 * ATTN_W_LOADS)
                if nxt:
                    add_output_bias(nxt)
                if prev:
                    second_norm(prev)
                if old:
                    dispatch(old)
                    rows_without_expert(old)
                    wait(pool, rows_sent[old.parity], old.turns(16 * TPG, 16 * TPG))
                    pool.sem_inc(rows_free, 1)

            pipeline(pool, step)

            pool.wait_ge(base_stored, 16 * (NG + 1))

            def send_rows(e, following):
                for c in range(SC):
                    if c == 0:
                        wait(pool, dest_ready, e.count(1, 1))
                    wait_alone(pool, y_ready, e.count(SC, c + 1))
                    pool.indirect_dma_start(out_rows, bass.IndirectOffsetOnAxis(ap=dest[e.parity][:, c:c + 1], axis=0),
                                            y_sb[e.parity][:, c, :], None, bounds_check=TOK - 1,
                                            oob_is_err=False).then_inc(y_sent[e.parity], 16)

            experts(pool, send_rows)
            for par in range(GPI):
                pool.wait_ge(y_sent[par], 16 * SC * E // GPI)

        @block.scalar
        def _(act):
            act.dma_start(ctx_sb[:, :, :], ctxT.rearrange("(k p) n -> p k n", p=P)).then_inc(kv_loaded, 16)
            act.dma_start(wk_sb[:, :, :], wkT.rearrange("(k p) n -> p k n", p=P)).then_inc(kv_loaded, 16)
            act.dma_start(bk_sb[:, :], bk[:, :]).then_inc(kv_loaded, 16)
            act.dma_start(wv_sb[:, :, :], wvT.rearrange("(k p) n -> p k n", p=P)).then_inc(kv_loaded, 16)
            act.dma_start(bv_sb[:, :], bv.rearrange("(a n) -> a n", a=1).broadcast_to([P, D])).then_inc(kv_loaded, 16)
            act.dma_start(mask_u8[:, :], mask.rearrange("(a b) k -> a (b k)", a=1)).then_inc(kv_loaded, 16)
            act.wait_ge(w_attn_loaded, 16 * ATTN_W_LOADS)

            def copy_xnT(s):
                for e in range(KD):
                    wait(act, xnT_ps, s.count(KD, e + 1))
                    act.copy(xnT[:, e, :], wk[e][:, :]).then_inc(xnT_ready, 1)

            def bias_queries(s):
                for m in range(KD):
                    wait(act, q_ps, s.count(KD, m + 1))
                    act.activation(qT[s.parity][:, m, :], wk[m][:, :], ACT.Identity,
                                   bias=bq_sb[:, m:m + 1]).then_inc(q_ready, 1)

            def exponentials(s, j):
                wait(act, shifted, s.count(TPG, j + 1))
                act.activation(probs[j % 2][:, 0:H * SK], probs[j % 2][:, 0:H * SK], ACT.Exp).then_inc(probs_ready, 1)

            def copy_probsT(s, j):
                for r, (c0, n) in enumerate(((0, 4), (4, 4), (8, 2))):
                    wait(act, probsT_ps, s.count(3 * TPG, 3 * j + r + 1))
                    act.copy(probsT[s.parity][:, c0:c0 + n, j * P:(j + 1) * P],
                             pt[r % 2][:, 0:n * P].rearrange("p (c q) -> p c q", c=n)).then_inc(probsT_ready, 1)

            def copy_attn(s, m):
                wait(act, attn_ps, s.count(KD, m + 1))
                wait(act, attnT_ready, s.count(KD, m - 1))
                act.copy(attnU[:, m, :], wk[0][:, :]).then_inc(attnU_ready, 1)

            def place_values(s):
                if isinstance(s.pair, int):
                    src = vblk[:, s.pair, :, :]
                else:
                    src = vblk[:, bass.ds(s.pair, 1), :, :].rearrange("p b c n -> p (b c) n")
                wait(act, v_placed, 16 * V_PARTS)
                wait(act, attn_ps, s.count(KD))
                act.copy(v_now[:, :, :], src).then_inc(v_now_ready, 1)

            def copy_tT(s):
                for k in range(KD):
                    wait(act, tT_ps, s.count(KD, k + 1))
                    act.copy(tT[:, k, :], wk[k][:, :]).then_inc(tT_ready, 1)

            def step(nxt, cur, prev, old):
                if old:
                    copy_tT(old)
                if prev:
                    copy_probsT(prev, TPG - 1)
                if cur:
                    exponentials(cur, 0)
                if prev:
                    copy_attn(prev, 0)
                if old:
                    wait(act, lgT_ps, old.count(1, 1))
                    act.copy(lgT[:, :], wk[1][:, :]).then_inc(lgT_ready, 1)
                if cur:
                    copy_probsT(cur, 0)
                    exponentials(cur, 1)
                if prev:
                    copy_attn(prev, 1)
                if old:
                    wait(act, lsh_ready, old.count(1, 1))
                    act.activation(lexp[:, :, :], lsh[:, :, :], ACT.Exp).then_inc(lexp_ready, 1)
                if cur:
                    copy_probsT(cur, 1)
                    exponentials(cur, 2)
                if nxt:
                    copy_xnT(nxt)
                if cur:
                    copy_probsT(cur, 2)
                    exponentials(cur, 3)
                if nxt:
                    bias_queries(nxt)
                if cur and cur.parity == 0:
                    place_values(cur)

            pipeline(act, step)

            def copy_tT_slots(e):
                wait(act, tT_slots_ps, e.count(3, 1))
                act.copy(tT_slots[:, 0, 0:4 * P], pt[0][:, :]).then_inc(tT_slots_ready, 1)
                wait(act, tT_slots_ps, e.count(3, 2))
                act.copy(tT_slots[:, 1, 0:4 * P], pt[1][:, :]).then_inc(tT_slots_ready, 1)
                wait(act, tT_slots_ps, e.count(3, 3))
                act.copy(tT_slots[:, :, 4 * P:5 * P],
                         pt[0][:, 0:KD * P].rearrange("p (k s) -> p k s", k=KD)).then_inc(tT_slots_ready, 1)

            copy_tT_slots(Stage(0, 0))

            def hidden_window(e, following):
                for f in range(FC):
                    wait(act, hidden_ps, e.count(2 * FC, 2 * f + 1))
                    act.activation(hidden[:, f, 0:CW], sc_ps[:, (2 * f) % 4, 0:CW], ACT.Relu).then_inc(hidden_ready[0], 1)
                if following:
                    copy_tT_slots(following)

            experts(act, hidden_window)

        @block.vector
        def _(dve):
            dve.wait_ge(kv_loaded, 16 * KV_LOADS)
            dve.wait_ge(consts_set, 2)
            dve.tensor_scalar(mask_row[0:1, :, :].rearrange("p b (h k) -> p b h k", h=HQ),
                              mask_u8[:, :].rearrange("p (b k) -> p b k", b=B)[:, :, None, :].broadcast_to([1, B, HQ, SK]),
                              MASKED, None, ALU.mult).then_inc(mask_ready, 1)
            for m in range(KD):
                dve.wait_ge(kT_ps, m + 1)
                dve.tensor_scalar(kT[:, m, :], wk[m][:, 0:B * SK], bk_sb[:, m:m + 1], float(DH) ** -0.5,
                                  ALU.add, ALU.mult).then_inc(kT_ready, 1)
            for i in range(B // 2):
                dve.wait_ge(v_ps, i + 1)
                dve.tensor_tensor(v_nat[:, 2 * i:2 * i + 2, :], pt[i][0:SK, :].rearrange("p (b n) -> p b n", b=2),
                                  bv_sb[0:SK, None, :].broadcast_to([SK, 2, D]), ALU.add).then_inc(v_nat_ready, 1)

            def first_moments(s):
                wait(dve, x_loaded[s.parity], s.turns(16, 16))
                wait(dve, moments1, s.count(1))
                for j in range(TPG):
                    last = dve.bn_stats(bn1[:, j, :], x_sb[:, group(s, j, 1), :].rearrange("p a d -> p (a d)"))
                last.then_inc(bn1_done, 1)
                wait_alone(dve, bn1_done, s.count(1, 1))
                for j in range(TPG):
                    last = dve.bn_aggr(mv1[:, j, :], bn1[:, j, :])
                last.then_inc(moments1, 1)

            def first_norm(s):
                wait(dve, rstd1_ready, s.count(1, 1))
                wait(dve, xnT_ps, s.count(KD))
                for j in range(TPG):
                    last = dve.tensor_scalar(xn[:, j:j + 1, :], x_sb[:, group(s, j, 1), :], mv1[:, j, 0:1], rstd1[:, j:j + 1],
                                             ALU.subtract, ALU.mult)
                last.then_inc(xn_ready, 1)

            def shift_scores(s, j):
                m = rowmax[:, j % 2, :]
                wait(dve, scores_ready, s.count(TPG, j + 1))
                dve.tensor_reduce(m, scores, AX.X, ALU.max).then_inc(rowmax_ready, 1)
                wait(dve, rowmax_ready, s.count(TPG, j + 1))
                wait(dve, probsT_ps, s.count(3 * TPG, 3 * (j - 1)))
                dve.tensor_tensor(probs[j % 2][:, 0:H * SK].rearrange("p (q h k) -> p q h k", q=4, h=HQ), scores,
                                  m.rearrange("p (q h) -> p q h", q=4)[:, :, :, None].broadcast_to([P, 4, HQ, SK]),
                                  ALU.subtract).then_inc(shifted, 1)

            def sum_probs(s, j):
                wait(dve, probs_ready, s.count(TPG, j + 1))
                if j == 0:
                    wait(dve, rsum_ready, s.count(1))
                dve.tensor_reduce(sums[:, j, :], probs[j % 2][:, 0:H * SK].rearrange("p (h k) -> p h k", h=H),
                                  AX.X, ALU.add).then_inc(sums_ready, 1)

            def invert_sums(s):
                wait(dve, sums_ready, s.count(TPG, TPG))
                wait(dve, rsum_wide_ready, s.count(1))
                dve.reciprocal(rsum[:, :, :], sums[:, :, :]).then_inc(rsum_ready, 1)

            def normalise_attn(s, m):
                wait(dve, attnU_ready, s.count(KD, m + 1))
                wait(dve, rsumT_ps, s.count(KD, m + 1))
                wait(dve, proj_ps, s.count(2))
                dve.tensor_tensor(attnT[:, m, :], attnU[:, m, :], pt[1 - m][:, :], ALU.mult).then_inc(attnT_ready, 1)

            def add_residual(s):
                r = rows[s.parity]
                wait(dve, xb_ready, s.count(1, 1))
                wait(dve, rows_free, s.count(1, 1))
                for h in range(2):
                    wait(dve, proj_ps, s.count(2, h + 1))
                    dve.tensor_tensor(r[:, 2 * h:2 * h + 2, 0:D], wk[h][:, :].rearrange("p (t d) -> p t d", t=2),
                                      x_sb[:, group(s, 2 * h, 2), :], ALU.add).then_inc(x1_ready, 1)

            def second_moments(s):
                r = rows[s.parity]
                wait(dve, x1_ready, s.count(2, 2))
                wait(dve, t_ready, s.count(1))
                for j in range(TPG):
                    last = dve.bn_stats(bn2[:, j, :], r[:, j, 0:D])
                last.then_inc(bn2_done, 1)
                wait_alone(dve, bn2_done, s.count(1, 1))
                for j in range(TPG):
                    last = dve.bn_aggr(mv2[:, j, :], bn2[:, j, :])
                last.then_inc(moments2, 1)

            def choose(s):
                def then(k, ins):
                    ins.then_inc(choice_step, 1)
                    dve.wait_ge(choice_step, s.count(3, k))
                logits = wk[1][:, :].rearrange("p (t c) -> p t c", t=TPG)[:, :, 0:E]
                wait(dve, logits_ps, s.count(1, 1))
                then(1, dve.tensor_reduce(lmax[:, :], logits, AX.X, ALU.max))
                dve.tensor_tensor(lsh[:, :, :], logits, lmax[:, :, None].broadcast_to([P, TPG, E]),
                                  ALU.subtract).then_inc(lsh_ready, 1)
                dve.wait_ge(lsh_ready, s.count(1, 1))
                then(2, dve.scalar_tensor_tensor(cand[:, :, :], lsh[:, :, :], 0.0, rank[:, :, :], ALU.is_equal, ALU.mult))
                then(3, dve.tensor_reduce(cmax[:, :], cand[:, :, :], AX.X, ALU.max))
                dve.tensor_tensor(onehot[:, :, :], cand[:, :, :], cmax[:, :, None].broadcast_to([P, TPG, E]),
                                  ALU.is_equal).then_inc(onehot_ready, 1)

            def place(s):
                def then(k, ins):
                    ins.then_inc(place_step, 1)
                    dve.wait_ge(place_step, s.count(3, k))
                r = rows[s.parity]
                wait(dve, prefix_ps, s.count(1, 1))
                dve.tensor_tensor(posm[:, :, :], wk[1][:, 0:TPG * E].rearrange("p (t e) -> p t e", t=TPG),
                                  onehot[:, :, :], ALU.mult).then_inc(posm_ready, 1)
                dve.tensor_reduce(group_taken[:, :], onehot[:, :, :].rearrange("p t e -> p e t"), AX.X, ALU.add)
                wait(dve, lexp_ready, s.count(1, 1))
                dve.tensor_reduce(esum[:, :], lexp[:, :, :], AX.X, ALU.add)
                wait(dve, base_ready, s.count(1, 1))
                then(1, dve.tensor_scalar(first[:, :], cmax[:, :], float(-CAP), float(E * CAP), ALU.mult, ALU.add))
                dve.tensor_tensor(taken[:, :], taken[:, :], group_taken[:, :], ALU.add).then_inc(taken_ready, 1)
                dve.reciprocal(pmax[:, :], esum[:, :])
                then(2, dve.tensor_reduce(pos[:, :], posm[:, :, :], AX.X, ALU.add))
                dve.tensor_scalar(keep[:, :], pos[:, :], float(CAP), None, ALU.is_lt)
                dve.tensor_scalar(past[:, :], pos[:, :], float(CAP), FAR, ALU.is_ge, ALU.mult)
                then(3, dve.tensor_tensor(slotf[:, :], first[:, :], pos[:, :], ALU.add))
                dve.tensor_tensor(slot[s.parity][:, :], slotf[:, :], past[:, :], ALU.add)
                dve.tensor_tensor(r[:, :, GATE], pmax[:, :], keep[:, :], ALU.mult)
                dve.tensor_copy(r[:, :, TOKEN], token_no[:, group(s)]).then_inc(route_ready, 1)

            def step(nxt, cur, prev, old):
                if cur:
                    shift_scores(cur, 0)
                if prev:
                    sum_probs(prev, TPG - 1)
                    invert_sums(prev)
                if nxt:
                    first_moments(nxt)
                if cur:
                    shift_scores(cur, 1)
                    sum_probs(cur, 0)
                if prev:
                    normalise_attn(prev, 0)
                if old:
                    choose(old)
                if prev:
                    normalise_attn(prev, 1)
                if nxt:
                    first_norm(nxt)
                if cur:
                    shift_scores(cur, 2)
                    sum_probs(cur, 1)
                if old:
                    place(old)
                if prev:
                    add_residual(prev)
                    second_moments(prev)
                if cur:
                    shift_scores(cur, 3)
                    sum_probs(cur, 2)

            pipeline(dve, step)

            def normalise_slots(e):
                r = srow[e.parity]
                wait(dve, srow_loaded[e.parity], e.turns(16, 16))
                wait(dve, tT_slots_ps, e.count(3))
                for c in range(SC):
                    last = dve.tensor_scalar(t_slots[:, c, :], r[:, c, 0:D], r[:, c, MEAN:MEAN + 1], r[:, c, RSTD:RSTD + 1],
                                             ALU.subtract, ALU.mult)
                last.then_inc(t_slots_ready, 1)
                wait(dve, y_sent[e.parity], e.turns(16 * SC))
                wait(dve, dest_ready, e.count(1))
                dve.tensor_scalar(empty[:, :], r[:, :, TOKEN], 0.0, FAR, ALU.is_equal, ALU.mult).then_inc(empty_ready, 1)
                dve.wait_ge(empty_ready, e.count(1, 1))
                dve.scalar_tensor_tensor(dest[e.parity][:, :], r[:, :, TOKEN], -1.0, empty[:, :],
                                         ALU.add, ALU.add).then_inc(dest_ready, 1)

            normalise_slots(Stage(0, 0))

            def expert_step(e, following):
                for f in range(FC):
                    if following and f == FC // 2:
                        normalise_slots(following)
                    wait(dve, hidden_ps, e.count(2 * FC, 2 * f + 2))
                    dve.tensor_scalar(hidden[:, f, CW:CAP], sc_ps[:, (2 * f + 1) % 4, 0:CW], 0.0, None,
                                      ALU.max).then_inc(hidden_ready[1], 1)
                for c in range(SC):
                    wait(dve, y_ps, e.count(SC, c + 1))
                    dve.scalar_tensor_tensor(y_sb[e.parity][:, c, :], wk[(SC * e.parity + c) % 2][:, 0:D],
                                             srow[e.parity][:, c, GATE:GATE + 1], srow[e.parity][:, c, 0:D],
                                             ALU.mult, ALU.add).then_inc(y_ready, 1)

            experts(dve, expert_step)

        @block.tensor
        def _(pe):
            pe.wait_ge(kv_loaded, 16 * KV_LOADS)
            for m in range(KD):
                for k in range(KD):
                    last = pe.matmul(wk[m][:, 0:B * SK], wk_sb[:, k, m * P:(m + 1) * P], ctx_sb[:, k, :],
                                     start=(k == 0), stop=(k == KD - 1))
                last.then_inc(kT_ps, 1)
            for b in range(B):
                for k in range(KD):
                    last = pe.matmul(pt[b // 2][0:SK, (b % 2) * D:(b % 2 + 1) * D], ctx_sb[:, k, b * SK:(b + 1) * SK],
                                     wv_sb[:, k, :], start=(k == 0), stop=(k == KD - 1))
                if b % 2:
                    last.then_inc(v_ps, 1)
            pe.wait_ge(consts_cut, 2)
            pe.wait_ge(kT_ready, KD)
            pe.wait_ge(v_nat_ready, B // 2)
            pe.wait_ge(w_attn_loaded, 16 * ATTN_W_LOADS)
            pe.wait_ge(mask_ready, 1)

            def transpose_xn(s):
                wait(pe, xn_ready, s.count(1, 1))
                wait(pe, x1_ready, s.count(2, -2))
                wait(pe, q_ready, s.count(KD))
                for k in range(KD):
                    for j in range(TPG):
                        last = pe.transpose(wk[k][:, j * P:(j + 1) * P], xn[:, j, k * P:(k + 1) * P], ident[:, :])
                    last.then_inc(xnT_ps, 1)

            def queries(s):
                wait(pe, xnT_ready, s.count(KD, KD))
                for m in range(KD):
                    for k in range(KD):
                        last = pe.matmul(wk[m][:, :], wq_sb[:, k, m * P:(m + 1) * P], xnT[:, k, :],
                                         start=(k == 0), stop=(k == KD - 1))
                    last.then_inc(q_ps, 1)

            def score(s, j):
                if j == 0:
                    wait(pe, q_ready, s.count(KD, KD))
                if isinstance(s.pair, int):
                    mrow, krow = mask_row[:, s.pair, :], kflat[:, s.pair, :, :]
                else:
                    mrow = mask_row[:, bass.ds(s.pair, 1), :].rearrange("p b c -> p (b c)")
                    krow = kflat[:, bass.ds(s.pair, 1), :, :].rearrange("p b m c -> p (b m) c")
                wait(pe, shifted, s.count(TPG, j))
                for q in range(4):
                    m, c = q // 2, (q % 2) * HQ * SK
                    pe.matmul(sc_ps[:, q, 0:HQ * SK], ones[:, :], mrow, start=True, stop=False)
                    last = pe.matmul(sc_ps[:, q, 0:HQ * SK], qT[s.parity][:, m, j * P:(j + 1) * P],
                                     krow[:, m, c:c + HQ * SK], start=False, stop=True)
                last.then_inc(scores_ready, 1)

            def transpose_probs(s, j):
                wait(pe, probs_ready, s.count(TPG, j + 1))
                if j == 1:
                    wait(pe, attnT_ready, s.count(KD))
                for r, (c0, n) in enumerate(((0, 4), (4, 4), (8, 2))):
                    wait(pe, probsT_ready, s.count(3 * TPG, 3 * j + (1 if r == 2 else 0)))
                    for i in range(n):
                        m, c = (c0 + i) // CH, (c0 + i) % CH
                        at = m * HH * SK + c * P
                        last = pe.transpose(pt[r % 2][:, i * P:(i + 1) * P], probs[j % 2][:, at:at + P], ident[:, :])
                    last.then_inc(probsT_ps, 1)

            def transpose_rsum(s, running):
                wait(pe, rsum_wide_ready, s.count(1, 1))
                wait(pe, probsT_ready, s.count(3 * TPG, 3 * TPG + (3 if running else 0)))
                for m in range(KD):
                    for j in range(TPG):
                        last = pe.transpose(pt[1 - m][:, j * P:(j + 1) * P], rsum_wide[:, j, m * P:(m + 1) * P], ident[:, :])
                    last.then_inc(rsumT_ps, 1)

            def weigh_values(s, m):
                if m == 0:
                    wait(pe, probsT_ready, s.count(3 * TPG, 3 * TPG))
                    wait(pe, v_now_ready, s.turns(1, 1))
                    wait(pe, tT_ready, s.count(KD))
                else:
                    wait(pe, attnU_ready, s.count(KD, 1))
                for c in range(CH):
                    last = pe.matmul(wk[0][:, :], v_now[:, m * CH + c, :], probsT[s.parity][:, m * CH + c, :],
                                     start=(c == 0), stop=(c == CH - 1))
                last.then_inc(attn_ps, 1)

            def project(s):
                wait(pe, attnT_ready, s.count(KD, KD))
                for h in range(2):
                    if h == 1:
                        wait(pe, posm_ready, s.count(1))
                    for j in range(2):
                        for m in range(KD):
                            last = pe.matmul(wk[h][:, j * D:(j + 1) * D], attnT[:, m, (2 * h + j) * P:(2 * h + j + 1) * P],
                                             wo_sb[:, m, :], start=(m == 0), stop=(m == KD - 1))
                    last.then_inc(proj_ps, 1)

            def transpose_t(s, ahead):
                wait(pe, t_ready, s.count(1, 1))
                wait(pe, q_ready, s.count(KD, KD + ahead * KD))
                for k in range(KD):
                    for j in range(TPG):
                        last = pe.transpose(wk[k][:, j * P:(j + 1) * P], t_sb[:, j, k * P:(k + 1) * P], ident[:, :])
                    last.then_inc(tT_ps, 1)

            def router_logits(s):
                wait(pe, tT_ready, s.count(KD, KD))
                for k in range(KD):
                    last = pe.matmul(wk[1][:, :], wr_sb[:, k, :], tT[:, k, :], start=(k == 0), stop=(k == KD - 1))
                last.then_inc(lgT_ps, 1)

            def transpose_logits(s):
                wait(pe, lgT_ready, s.count(1, 1))
                for j in range(TPG):
                    last = pe.transpose(wk[1][:, j * P:(j + 1) * P], lgT[:, j * P:(j + 1) * P], ident[:, :])
                last.then_inc(logits_ps, 1)

            def count_before(s):
                wait(pe, onehot_ready, s.count(1, 1))
                wait(pe, taken_ready, s.count(1, 1))
                dst = wk[1][:, 0:TPG * E]
                pe.matmul(dst, before[:, :], onehot[:, :, :], start=True, stop=False)
                for j in range(TPG):
                    pe.matmul(wk[1][:, j * E:(j + 1) * E], ones[:, :], taken[:, :], start=False, stop=False)
                for j in range(1, TPG):
                    for i in range(j):
                        last = pe.matmul(wk[1][:, j * E:(j + 1) * E], ones[:, :], onehot[:, i, :], start=False,
                                         stop=(j == TPG - 1 and i == j - 1))
                last.then_inc(prefix_ps, 1)

            def step(nxt, cur, prev, old):
                if cur:
                    if cur.parity == 0:
                        wait(pe, kblk_ready, cur.turns(KD, KD))
                    score(cur, 0)
                if old:
                    transpose_t(old, 2 if cur else 1 if prev else 0)
                if prev:
                    transpose_probs(prev, TPG - 1)
                    weigh_values(prev, 0)
                if old:
                    router_logits(old)
                if cur:
                    score(cur, 1)
                    transpose_probs(cur, 0)
                if old:
                    transpose_logits(old)
                if prev:
                    transpose_rsum(prev, cur is not None)
                    weigh_values(prev, 1)
                if cur:
                    score(cur, 2)
                if old:
                    count_before(old)
                if cur:
                    transpose_probs(cur, 1)
                if prev:
                    project(prev)
                if cur:
                    score(cur, 3)
                if nxt:
                    transpose_xn(nxt)
                if cur:
                    transpose_probs(cur, 2)
                if nxt:
                    queries(nxt)

            pipeline(pe, step)

            def transpose_slots(e):
                wait(pe, t_slots_ready, e.count(1, 1))
                wait(pe, tT_slots_ready, e.count(3))
                for k in range(KD):
                    for c in range(4):
                        last = pe.transpose(pt[k][:, c * P:(c + 1) * P], t_slots[:, c, k * P:(k + 1) * P], ident[:, :])
                    last.then_inc(tT_slots_ps, 1)
                wait(pe, tT_slots_ready, e.count(3, 1))
                for k in range(KD):
                    last = pe.transpose(pt[0][:, k * P:(k + 1) * P], t_slots[:, 4, k * P:(k + 1) * P], ident[:, :])
                last.then_inc(tT_slots_ps, 1)

            transpose_slots(Stage(0, 0))

            def expert_step(e, following):
                wait(pe, w_loaded[e.parity], e.turns(32, 32))
                wait(pe, tT_slots_ready, e.count(3, 3))
                for f in range(FC):
                    for w in range(2):
                        wait(pe, hidden_ready[w], e.count(FC, f - 1))
                        for k in range(KD):
                            last = pe.matmul(sc_ps[:, (2 * f + w) % 4, 0:CW], w1_sb[e.parity][:, k, f * P:(f + 1) * P],
                                             tT_slots[:, k, w * CW:(w + 1) * CW], start=(k == 0), stop=(k == KD - 1))
                        last.then_inc(hidden_ps, 1)
                if following:
                    transpose_slots(following)
                for w in range(2):
                    wait(pe, hidden_ready[w], e.count(FC, FC))
                for c in range(SC):
                    wait(pe, y_ready, e.count(SC, c - 1))
                    for f in range(FC):
                        last = pe.matmul(wk[(SC * e.parity + c) % 2][:, 0:D], hidden[:, f, c * P:(c + 1) * P],
                                         w2_sb[e.parity][:, f, :], start=(f == 0), stop=(f == FC - 1))
                    last.then_inc(y_ps, 1)

            experts(pe, expert_step)


def kernel(x, ctx_1024, mask_BxS2_bk0, L0_xattn_Wq, L0_xattn_bq, L0_xattn_Wk, L0_xattn_bk, L0_xattn_Wv, L0_xattn_bv,
           L0_xattn_Wo, L0_xattn_bo, L0_ffn_Wr, L0_ffn_W1, L0_ffn_W2):
    import concourse.bacc as bacc
    from concourse.bass_utils import run_bass_kernel_spmd

    arrays = {
        "in_x": np.asarray(x),
        "in_ctxT": np.asarray(ctx_1024).reshape(B * SK, D).T,
        "in_mask": np.asarray(mask_BxS2_bk0),
        "in_wqT": np.asarray(L0_xattn_Wq).T, "in_bq": np.asarray(L0_xattn_bq).reshape(KD, P).T,
        "in_wkT": np.asarray(L0_xattn_Wk).T, "in_bk": np.asarray(L0_xattn_bk).reshape(KD, P).T,
        "in_wvT": np.asarray(L0_xattn_Wv).T, "in_bv": np.asarray(L0_xattn_bv),
        "in_woT": np.asarray(L0_xattn_Wo).T, "in_bo": np.asarray(L0_xattn_bo),
        "in_wr": np.asarray(L0_ffn_Wr), "in_w1": np.asarray(L0_ffn_W1), "in_w2": np.asarray(L0_ffn_W2),
    }
    arrays = {name: np.ascontiguousarray(a) for name, a in arrays.items()}
    nc = bacc.Bacc("TRN2", target_bir_lowering=False, num_devices=1)
    args = [nc.dram_tensor(name, a.shape, mybir.dt.from_np(a.dtype), kind="ExternalInput").ap() for name, a in arrays.items()]
    args.append(nc.dram_tensor("out_x", (B, S, D), F32, kind="ExternalOutput").ap())
    xattn_moe(nc, *args)
    r = run_bass_kernel_spmd(nc, [arrays], core_ids=[0])
    return r.results[0]["out_x"]
```

```python
from contextlib import ExitStack

import numpy as np

import concourse.bass as bass
from concourse import mybir
from concourse.alu_op_type import AluOpType as ALU

F32 = mybir.dt.float32
BF16 = mybir.dt.bfloat16
I32 = mybir.dt.int32
U8 = mybir.dt.uint8
ACT = mybir.ActivationFunctionType
AX = mybir.AxisListType

P = 128
B, S, D = 4, 1024, 256
H = 16
DH = D // H
SK = 77
E, FF = 8, 1024
TOK = B * S
CAP = int(1.25 * TOK / E)
KD = D // P
HH = H // KD
HQ = HH // 2
TPG = 4
GT = TPG * P
NG = TOK // GT
GPB = S // GT
CH = -(-HH * SK // P)
PAD = (CH * P - HH * SK)
FC = FF // P
SC = CAP // P
MIN_TILES = 2
BANK = 512
ROW = D + 4
ROUNDS = ((0, 4), (4, 4), (8, 2))
MEAN, RSTD, GATE, TOKEN = D, D + 1, D + 2, D + 3
EPS = 1e-5
MASKED = -3.0e38
PE_MASKED = (3,)
FAR = 65536.0
GPI = 2


def wait(eng, sem, value):
    if isinstance(value, int) and value <= 0:
        return
    eng.wait_ge(sem, value)


class Stage:

    def __init__(self, pair, parity):
        self.pair, self.parity = pair, parity

    def count(self, per, more=0):
        if isinstance(self.pair, int):
            return per * (GPI * self.pair + self.parity) + more
        return self.pair * (GPI * per) + (per * self.parity + more)

    def turns(self, per, more=0):
        return self.pair * per + more


def pipeline(eng, step):

    def at(g):
        return Stage(g // GPI, g % GPI) if 0 <= g < NG else None

    def peeled(g):
        step(at(g + 1), at(g), at(g - 1), at(g - 2))

    for g in range(-1, GPI):
        peeled(g)
    with eng.Fori(1, NG // GPI - 1) as pair:
        for par in range(GPI):
            stages = []
            for lag in (-1, 0, 1, 2):
                q = (par - lag) % GPI
                stages.append(Stage(pair + (par - lag - q) // GPI, q))
            step(*stages)
    for g in range(NG - GPI, NG + 2):
        peeled(g)


def experts(eng, step):
    step(Stage(0, 0), Stage(0, 1))
    step(Stage(0, 1), Stage(1, 0))
    with eng.Fori(1, E // GPI - 1) as pair:
        step(Stage(pair, 0), Stage(pair, 1))
        step(Stage(pair, 1), Stage(pair + 1, 0))
    step(Stage(E // GPI - 1, 0), Stage(E // GPI - 1, 1))
    step(Stage(E // GPI - 1, 1), None)


def windows_of(tiles):
    windows = -(-tiles * P // BANK)
    return tiles * P // windows, windows


def skipped_too(c, tiles):
    return 1 if c < tiles - 1 else SC - tiles + 1


def xattn_moe(nc, x, ctxT, mask, wqT, bq, wkT, bk, wvT, bv, woT, bo, wr, w1, w2, out):
    ctx = ExitStack()
    with ctx:
        def sb(name, shape, dt=F32):
            return ctx.enter_context(nc.sbuf_tensor(name, shape, dt))

        def sem(name):
            return ctx.enter_context(nc.semaphore(name))

        slots_dram = nc.dram_tensor("slot_rows", (E * CAP, ROW), F32, kind="Internal").ap()

        ident = sb("ident", [P, P])
        before = sb("before", [P, P], BF16)
        ones = sb("ones", [P, P], BF16)
        headmask = sb("headmask", [P, HH])
        zeros = sb("zeros", [P, ROW])
        token_no = sb("token_no", [P, TOK // P])
        rank = sb("rank", [P, TPG, E])
        neg_half = sb("neg_half", [P, TPG])
        wq_sb = sb("wq_sb", [P, KD, D])
        wk_sb = sb("wk_sb", [P, KD, D])
        wv_sb = sb("wv_sb", [P, KD, D])
        wo_sb = sb("wo_sb", [P, KD, D])
        wr_sb = sb("wr_sb", [P, KD, P])
        bq_sb = sb("bq_sb", [P, KD])
        bk_sb = sb("bk_sb", [P, KD])
        bv_sb = sb("bv_sb", [P, D])
        bo_sb = sb("bo_sb", [P, D])
        ctx_sb = sb("ctx_sb", [P, KD, B * SK])
        mask_u8 = sb("mask_u8", [P, B * SK], U8)
        mask_add = sb("mask_add", [P, B, SK])
        mask_row = sb("mask_row", [P, B, HQ * SK], BF16)

        x_sb = sb("x_sb", [P, TOK // P, D])
        kT = sb("kT", [P, KD, B * SK])
        kblk_mem = sb("kblk_mem", [P, B * KD * HH * SK])
        v_nat = sb("v_nat", [SK, B, D])
        vblk_mem = sb("vblk_mem", [P, B * KD * CH * P])
        v_now = sb("v_now", [P, KD * CH, P])
        xn = sb("xn", [P, TPG, D])
        xnT = sb("xnT", [P, KD, GT])
        qT = [sb(f"qT{i}", [P, KD, GT]) for i in range(GPI)]
        probs = [sb(f"probs{i}", [P, H * SK + PAD]) for i in range(2)]
        rowmax = sb("rowmax", [P, 2, H])
        sums = sb("sums", [P, TPG, H])
        rsum = sb("rsum", [P, TPG, H])
        rsum_wide = sb("rsum_wide", [P, TPG, D])
        probsT_mem = [sb(f"probsT{i}", [P, KD * CH * GT]) for i in range(GPI)]
        attnU = sb("attnU", [P, KD, GT])
        attnT = sb("attnT", [P, KD, GT])
        rows = [sb(f"rows{i}", [P, TPG, ROW]) for i in range(GPI)]
        t_sb = sb("t_sb", [P, TPG, D])
        tT = sb("tT", [P, KD, GT])
        base = sb("base", [P, TPG, D])
        bn1 = sb("bn1", [P, TPG, 6])
        mv1 = sb("mv1", [P, TPG, 2])
        bn2 = sb("bn2", [P, TPG, 6])
        mv2 = sb("mv2", [P, TPG, 2])
        var1, y1, yy1, rstd1 = (sb(f"ln1_{i}", [P, TPG]) for i in range(4))
        var2, y2, yy2, rstd2 = (sb(f"ln2_{i}", [P, TPG]) for i in range(4))

        lgT = sb("lgT", [P, GT])
        lmax = sb("lmax", [P, TPG])
        lsh = sb("lsh", [P, TPG, E])
        lexp = sb("lexp", [P, TPG, E])
        cand = sb("cand", [P, TPG, E])
        cmax = sb("cmax", [P, TPG])
        onehot = sb("onehot", [P, TPG, E], BF16)
        taken = sb("taken", [P, E], BF16)
        group_taken = sb("group_taken", [P, E])
        posm = sb("posm", [P, TPG, E])
        pos = sb("pos", [P, TPG])
        keep = sb("keep", [P, TPG])
        esum = sb("esum", [P, TPG])
        pmax = sb("pmax", [P, TPG])
        past = sb("past", [P, TPG])
        first = sb("first", [P, TPG])
        slotf = sb("slotf", [P, TPG])
        slot = [sb(f"slot{i}", [P, TPG], I32) for i in range(GPI)]
        drop, drs, scale_b, shift_b = (sb(f"base_{i}", [P, TPG]) for i in range(4))

        kblk = kblk_mem[:, :].rearrange("p (b m h k) -> p b m h k", b=B, m=KD, h=HH)
        kflat = kblk_mem[:, :].rearrange("p (b m c) -> p b m c", b=B, m=KD)
        vblk = vblk_mem[:, :].rearrange("p (b c n) -> p b c n", b=B, c=KD * CH)
        probsT = [t[:, :].rearrange("p (c n) -> p c n", c=KD * CH) for t in probsT_mem]
        w_mem = [vblk_mem, kblk_mem]
        w1_sb = [m[:, 0:KD * FF].rearrange("p (k f) -> p k f", k=KD) for m in w_mem]
        w2_sb = [m[:, KD * FF:KD * FF + FC * D].rearrange("p (c d) -> p c d", c=FC) for m in w_mem]
        hidden = probsT_mem[0][:, 0:FC * CAP].rearrange("p (c s) -> p c s", c=FC)
        spare = probsT_mem[1]
        t_slots = spare[:, 0:SC * D].rearrange("p (s d) -> p s d", s=SC)
        tT_slots = spare[:, SC * D:2 * SC * D].rearrange("p (k s) -> p k s", k=KD)
        y_sb = [spare[:, (2 + i) * SC * D:(3 + i) * SC * D].rearrange("p (s d) -> p s d", s=SC) for i in range(GPI)]
        x_flat = x_sb[:, :, :].rearrange("p t d -> p (t d)")
        srow = [x_flat[:, i * SC * ROW:(i + 1) * SC * ROW].rearrange("p (s r) -> p s r", s=SC) for i in range(GPI)]
        empty = sb("empty", [P, SC])
        tiles_f = [sb(f"tiles_f{i}", [P, E]) for i in range(2)]
        tiles_used = sb("tiles_used", [P, E], I32)
        dest = [sb(f"dest{i}", [P, SC], I32) for i in range(GPI)]

        sc_ps = ctx.enter_context(nc.psum_tensor("sc_ps", [P, 4, 512], F32))
        pt = [ctx.enter_context(nc.psum_tensor(f"pt{i}", [P, 512], F32)) for i in range(2)]
        wk = [ctx.enter_context(nc.psum_tensor(f"wk{i}", [P, 512], F32)) for i in range(2)]
        scores = sc_ps[:, :, 0:HQ * SK].rearrange("p q (h k) -> p q h k", h=HQ)

        k_loaded = sem("k_loaded")
        v_loaded = sem("v_loaded")
        wq_loaded = sem("wq_loaded")
        w_attn_loaded = sem("w_attn_loaded")
        x_loaded = [sem(f"x_loaded{i}") for i in range(GPI)]
        v_placed = sem("v_placed")
        slots_zeroed = sem("slots_zeroed")
        rows_free = sem("rows_free")
        rows_sent = [sem(f"rows_sent{i}") for i in range(GPI)]
        base_stored = sem("base_stored")
        w_loaded = [sem(f"w_loaded{i}") for i in range(GPI)]
        srow_loaded = [sem(f"srow_loaded{i}") for i in range(GPI)]
        y_sent = [sem(f"y_sent{i}") for i in range(GPI)]
        consts_set = sem("consts_set")
        consts_cut = sem("consts_cut")
        mask_ready = sem("mask_ready")
        kT_ps = sem("kT_ps")
        kT_ready = sem("kT_ready")
        kblk_ready = sem("kblk_ready")
        v_ps = sem("v_ps")
        v_nat_ready = sem("v_nat_ready")
        vblk_zeroed = sem("vblk_zeroed")
        v_now_ready = sem("v_now_ready")
        bn1_done = sem("bn1_done")
        moments1 = sem("moments1")
        rstd1_step = sem("rstd1_step")
        rstd1_ready = sem("rstd1_ready")
        xn_ready = sem("xn_ready")
        xb_ready = sem("xb_ready")
        xnT_ps = sem("xnT_ps")
        xnT_ready = sem("xnT_ready")
        q_ps = sem("q_ps")
        q_ready = sem("q_ready")
        scores_ready = sem("scores_ready")
        scores_read = sem("scores_read")
        rowmax_ready = sem("rowmax_ready")
        shifted = sem("shifted")
        probs_ready = sem("probs_ready")
        sums_ready = sem("sums_ready")
        rsum_ready = sem("rsum_ready")
        probsT_ps = sem("probsT_ps")
        probsT_ready = sem("probsT_ready")
        rsum_wide_ready = sem("rsum_wide_ready")
        rsumT_ps = sem("rsumT_ps")
        attn_ps = sem("attn_ps")
        attnU_ready = sem("attnU_ready")
        attnT_ready = sem("attnT_ready")
        proj_ps = sem("proj_ps")
        x1_ready = sem("x1_ready")
        bn2_done = sem("bn2_done")
        moments2 = sem("moments2")
        rstd2_step = sem("rstd2_step")
        t_ready = sem("t_ready")
        tT_ps = sem("tT_ps")
        tT_ready = sem("tT_ready")
        lgT_ps = sem("lgT_ps")
        lgT_ready = sem("lgT_ready")
        logits_ps = sem("logits_ps")
        choice_step = sem("choice_step")
        lsh_ready = sem("lsh_ready")
        lexp_ready = sem("lexp_ready")
        onehot_ready = sem("onehot_ready")
        taken_ready = sem("taken_ready")
        prefix_ps = sem("prefix_ps")
        posm_ready = sem("posm_ready")
        place_step = sem("place_step")
        route_ready = sem("route_ready")
        base_step = sem("base_step")
        scales_ready = sem("scales_ready")
        base_ready = sem("base_ready")
        totals_ps = sem("totals_ps")
        tiles_step = sem("tiles_step")
        tiles_ready = sem("tiles_ready")
        t_slots_ready = sem("t_slots_ready")
        empty_ready = sem("empty_ready")
        dest_ready = sem("dest_ready")
        tT_slots_ps = sem("tT_slots_ps")
        tT_slots_ready = sem("tT_slots_ready")
        hidden_ps = sem("hidden_ps")
        hidden_ready = [sem(f"hidden_ready{i}") for i in range(2)]
        y_ps = sem("y_ps")
        y_ready = sem("y_ready")

        x_tiles = x.rearrange("b s d -> (b s) d").rearrange("(t p) d -> p t d", p=P)
        out_rows = out.rearrange("b s d -> (b s) d")
        out_tiles = out_rows.rearrange("(t p) d -> p t d", p=P)
        V_PARTS = KD * (HH + sum(1 for h in range(HH) if h * SK // P != ((h + 1) * SK - 1) // P))
        WQ_LOADS = 2
        ATTN_W_LOADS = 3
        K_LOADS = 3
        V_LOADS = 3

        def group(s, j=0, n=TPG):
            if isinstance(s.pair, int):
                t = TPG * (GPI * s.pair + s.parity) + j
                return slice(t, t + n)
            return bass.ds(s.pair * (GPI * TPG) + (TPG * s.parity + j), n)

        def by_tiles(eng, e, body):
            if isinstance(e.pair, int):
                n = GPI * e.pair + e.parity
                cell = tiles_used[0:1, n:n + 1]
            else:
                cell = tiles_used[0:1, bass.ds(e.pair * GPI + e.parity, 1)]
            used = eng.value_load(cell, min_val=MIN_TILES, max_val=SC)
            for tiles in range(MIN_TILES, SC + 1):
                with eng.If(used == tiles):
                    body(tiles)

        block = ctx.enter_context(nc.Block())

        waits_passed = sem("waits_passed")

        def wait_alone(eng, sem, value):
            wait(eng, sem, value)
            if not isinstance(value, int):
                eng.sem_inc(waits_passed, 1)

        @block.sync
        def _(sp):
            def load_x(s):
                wait(sp, x_loaded[s.parity], s.turns(16))
                sp.dma_start(x_sb[:, group(s), :], x_tiles[:, group(s), :]).then_inc(x_loaded[s.parity], 16)

            sp.sem_inc(base_stored, 16)
            load_x(Stage(0, 0))
            sp.dma_start(wq_sb[:, :, :], wqT.rearrange("(k p) n -> p k n", p=P)).then_inc(wq_loaded, 16)
            sp.dma_start(bq_sb[:, :], bq[:, :]).then_inc(wq_loaded, 16)
            sp.dma_start(wo_sb[:, :, :], woT.rearrange("(k p) n -> p k n", p=P)).then_inc(w_attn_loaded, 16)
            sp.dma_start(bo_sb[:, :], bo.rearrange("(a n) -> a n", a=1).broadcast_to([P, D])).then_inc(w_attn_loaded, 16)
            sp.wait_ge(consts_set, 1)
            sp.dma_start(wr_sb[:, :, 0:E], wr.rearrange("(k p) e -> p k e", p=P)).then_inc(w_attn_loaded, 16)
            load_x(Stage(0, 1))
            with sp.Fori(1, NG // GPI) as pair:
                for par in range(GPI):
                    load_x(Stage(pair, par))
            sp.wait_ge(v_nat_ready, B // 2)
            sp.wait_ge(vblk_zeroed, 1)
            for h in range(HH):
                r = h * SK
                while r < (h + 1) * SK:
                    end = min((h + 1) * SK, (r // P + 1) * P)
                    for m in range(KD):
                        c, k0 = m * CH + r // P, r - h * SK
                        cols = (m * HH + h) * DH
                        sp.dma_start(vblk[r % P:r % P + end - r, :, c, h * DH:(h + 1) * DH],
                                     v_nat[k0:k0 + end - r, :, cols:cols + DH]).then_inc(v_placed, 16)
                    r = end
            sp.wait_ge(consts_set, 1)
            sp.dma_start(slots_dram.rearrange("(p s) r -> p s r", p=P),
                         zeros[:, None, :].broadcast_to([P, E * CAP // P, ROW])).then_inc(slots_zeroed, 16)

            def load_weights(e, number):
                sp.dma_start(w1_sb[e.parity], w1[number].rearrange("e (k p) f -> p (e k) f", p=P)).then_inc(w_loaded[e.parity], 16)
                sp.dma_start(w2_sb[e.parity], w2[number].rearrange("e (c p) d -> p (e c) d", p=P)).then_inc(w_loaded[e.parity], 16)

            def step(nxt, cur, prev, old):
                number = GPI * old.pair + old.parity if old and isinstance(old.pair, int) else None
                if number == NG - 3:
                    sp.wait_ge(v_now_ready, B)
                    load_weights(Stage(0, 0), slice(0, 1))
                if number == NG - 2:
                    sp.wait_ge(scores_ready, TOK // P)
                    load_weights(Stage(0, 1), slice(1, 2))
                if number == NG - 1:
                    for par in range(GPI):
                        sp.wait_ge(rows_sent[par], 16 * TOK // P // GPI)
                    for par in range(GPI):
                        load_slots(Stage(0, par))
                if old:
                    wait(sp, base_ready, old.count(1, 2))
                    sp.dma_start(out_tiles[:, group(old), :], base[:, :, :]).then_inc(base_stored, 16)

            def load_slots(e):
                if isinstance(e.pair, int):
                    n = (GPI * e.pair + e.parity) * CAP
                    src = slots_dram[n:n + CAP, :]
                else:
                    src = slots_dram[bass.ds(e.pair * (GPI * CAP) + e.parity * CAP, CAP), :]
                wait(sp, y_ready, e.count(SC, -SC))
                sp.dma_start(srow[e.parity], src.rearrange("(s p) r -> p s r", p=P)).then_inc(srow_loaded[e.parity], 16)

            pipeline(sp, step)
            with sp.Fori(1, E // GPI) as pair:
                for par in range(GPI):
                    e = Stage(pair, par)
                    load_slots(e)
                    wait(sp, y_ps, e.count(SC, -SC))
                    load_weights(e, bass.ds(pair * GPI + par, 1))
            sp.wait_ge(base_stored, 16 * (NG + 1))

        @block.gpsimd
        def _(pool):
            pool.sem_inc(rows_free, GPI)
            pool.sem_inc(scales_ready, 1)
            pool.sem_inc(base_ready, 1)
            pool.memset(zeros[:, :], 0.0)
            pool.memset(wr_sb[:, :, :], 0.0).then_inc(consts_set, 1)
            pool.memset(ident[:, :], 1.0)
            pool.memset(before[:, :], 1.0)
            pool.memset(ones[:, :], 1.0)
            pool.memset(headmask[:, :], 1.0)
            pool.memset(taken[:, :], 0.0).then_inc(taken_ready, 1)
            for q in probs:
                pool.memset(q[:, H * SK:], 0.0)
            pool.memset(neg_half[:, :], -0.5)
            pool.memset(mask_row[:, :, :], 0.0).then_inc(consts_set, 1)
            pool.wait_ge(consts_set, 2)
            pool.affine_select(out=ident[:, :], in_=ident[:, :], compare_op=ALU.is_equal, fill=0.0,
                               base=0, pattern=[[-1, P]], channel_multiplier=1)
            pool.affine_select(out=before[:, :], in_=before[:, :], compare_op=ALU.is_gt, fill=0.0,
                               base=0, pattern=[[1, P]], channel_multiplier=-1)
            pool.iota(token_no[:, :], [[P, TOK // P]], base=1, channel_multiplier=1,
                      allow_small_or_imprecise_dtypes=True)
            pool.iota(rank[:, :, :], [[0, TPG], [-1, E]], base=E, channel_multiplier=0,
                      allow_small_or_imprecise_dtypes=True)
            pool.affine_select(out=headmask[:, :], in_=headmask[:, :], compare_op=ALU.is_ge, fill=0.0,
                               base=0, pattern=[[-DH, HH]], channel_multiplier=1).then_inc(consts_cut, 1)
            pool.wait_ge(consts_cut, 1)
            pool.affine_select(out=headmask[:, :], in_=headmask[:, :], compare_op=ALU.is_ge, fill=0.0,
                               base=DH - 1, pattern=[[DH, HH]], channel_multiplier=-1).then_inc(consts_cut, 1)

            def inverse_std(s, var, moments, y, yy, result, step, steps, mv):
                def then(k, ins):
                    ins.then_inc(step, 1)
                    (wait_alone if k == 4 else wait)(pool, step, s.count(steps, k))
                wait_alone(pool, moments, s.count(1, 1))
                then(1, pool.tensor_scalar(var[:, :], mv[:, :, 1], EPS, None, ALU.add))
                then(2, pool.tensor_tensor(y[:, :], var[:, :], neg_half[:, :], ALU.pow))
                then(3, pool.tensor_tensor(yy[:, :], y[:, :], y[:, :], ALU.mult))
                then(4, pool.tensor_tensor(yy[:, :], yy[:, :], var[:, :], ALU.mult))
                then(5, pool.tensor_scalar(yy[:, :], yy[:, :], -0.5, 1.5, ALU.mult, ALU.add))
                return pool.tensor_tensor(result, y[:, :], yy[:, :], ALU.mult)

            def rstd_first(s):
                wait(pool, xn_ready, s.count(1))
                inverse_std(s, var1, moments1, y1, yy1, rstd1[:, :], rstd1_step, 5, mv1).then_inc(rstd1_ready, 1)

            def spread_rsum(s):
                wait(pool, rsum_ready, s.count(1, 1))
                wait_alone(pool, rsumT_ps, s.count(KD))
                pool.tensor_copy(rsum_wide[:, :, :].rearrange("p t (h d) -> p t h d", h=H),
                                 rsum[:, :, :, None].broadcast_to([P, TPG, H, DH])).then_inc(rsum_wide_ready, 1)

            def add_output_bias(s):
                wait(pool, xn_ready, s.count(1, 1))
                pool.tensor_tensor(x_sb[:, group(s), :], x_sb[:, group(s), :],
                                   bo_sb[:, None, :].broadcast_to([P, TPG, D]), ALU.add).then_inc(xb_ready, 1)

            def second_rstd(s):
                r = rows[s.parity]
                inverse_std(s, var2, moments2, y2, yy2, rstd2[:, :], rstd2_step, 8, mv2).then_inc(rstd2_step, 1)
                wait_alone(pool, rstd2_step, s.count(8, 6))
                pool.tensor_copy(r[:, :, RSTD], rstd2[:, :]).then_inc(rstd2_step, 1)
                pool.tensor_copy(r[:, :, MEAN], mv2[:, :, 0]).then_inc(rstd2_step, 1)

            def base_scales(s):
                r = rows[s.parity]
                wait_alone(pool, base_ready, s.count(1, 1))
                pool.tensor_scalar(drop[:, :], keep[:, :], 1.0, None, ALU.subtract).then_inc(base_step, 1)
                pool.wait_ge(base_step, s.count(2, 1))
                pool.tensor_tensor(drs[:, :], drop[:, :], r[:, :, RSTD], ALU.mult).then_inc(base_step, 1)
                wait_alone(pool, base_step, s.count(2, 2))
                pool.tensor_scalar(scale_b[:, :], drs[:, :], -1.0, 1.0, ALU.mult, ALU.add)
                pool.tensor_tensor(shift_b[:, :], drs[:, :], r[:, :, MEAN], ALU.mult).then_inc(scales_ready, 1)

            def rows_without_expert(s):
                wait_alone(pool, scales_ready, s.count(1, 2))
                wait_alone(pool, base_stored, s.count(16, 16))
                for j in range(TPG):
                    last = pool.tensor_scalar(base[:, j, :], rows[s.parity][:, j, 0:D], scale_b[:, j:j + 1], shift_b[:, j:j + 1],
                                              ALU.mult, ALU.add)
                last.then_inc(base_ready, 1)

            def dispatch(s):
                wait_alone(pool, route_ready, s.count(1, 1))
                for j in range(TPG):
                    pool.indirect_dma_start(slots_dram, bass.IndirectOffsetOnAxis(ap=slot[s.parity][:, j:j + 1], axis=0),
                                            rows[s.parity][:, j, :], None, bounds_check=E * CAP - 1,
                                            oob_is_err=False).then_inc(rows_sent[s.parity], 16)

            def step(nxt, cur, prev, old):
                if prev and old is None:
                    pool.wait_ge(slots_zeroed, 16)
                if prev:
                    spread_rsum(prev)
                if nxt:
                    rstd_first(nxt)
                if cur is None and nxt:
                    for b in range(B):
                        for m in range(KD):
                            if b == 0 and m == 0:
                                pool.wait_ge(kT_ready, KD)
                            pool.tensor_tensor(
                                kblk[:, b, m, :, :],
                                kT[:, m, b * SK:(b + 1) * SK][:, None, :].broadcast_to([P, HH, SK]),
                                headmask[:, :][:, :, None].broadcast_to([P, HH, SK]), ALU.mult).then_inc(kblk_ready, 1)
                    pool.memset(vblk_mem[:, :], 0.0).then_inc(vblk_zeroed, 1)
                    pool.wait_ge(w_attn_loaded, 16 * ATTN_W_LOADS)
                if nxt:
                    add_output_bias(nxt)
                if old:
                    dispatch(old)
                    base_scales(old)
                if prev:
                    second_rstd(prev)
                if old:
                    rows_without_expert(old)
                    wait(pool, rows_sent[old.parity], old.turns(16 * TPG, 16 * TPG))
                    pool.sem_inc(rows_free, 1)

            pipeline(pool, step)

            pool.wait_ge(base_stored, 16 * (NG + 1))

            def send_rows(e, following):
                for c in range(SC):
                    if c == 0:
                        wait(pool, dest_ready, e.count(1, 1))
                    wait_alone(pool, y_ready, e.count(SC, c + 1))
                    pool.indirect_dma_start(out_rows, bass.IndirectOffsetOnAxis(ap=dest[e.parity][:, c:c + 1], axis=0),
                                            y_sb[e.parity][:, c, :], None, bounds_check=TOK - 1,
                                            oob_is_err=False).then_inc(y_sent[e.parity], 16)

            experts(pool, send_rows)
            for par in range(GPI):
                pool.wait_ge(y_sent[par], 16 * SC * E // GPI)

        @block.scalar
        def _(act):
            act.dma_start(ctx_sb[:, :, :], ctxT.rearrange("(k p) n -> p k n", p=P)).then_inc(k_loaded, 16)
            act.dma_start(wk_sb[:, :, :], wkT.rearrange("(k p) n -> p k n", p=P)).then_inc(k_loaded, 16)
            act.dma_start(bk_sb[:, :], bk[:, :]).then_inc(k_loaded, 16)
            act.dma_start(wv_sb[:, :, :], wvT.rearrange("(k p) n -> p k n", p=P)).then_inc(v_loaded, 16)
            act.dma_start(bv_sb[:, :], bv.rearrange("(a n) -> a n", a=1).broadcast_to([P, D])).then_inc(v_loaded, 16)
            act.dma_start(mask_u8[:, :], mask.rearrange("(a b) k -> a (b k)", a=1).broadcast_to([P, B * SK])).then_inc(v_loaded, 16)

            def copy_xnT(s):
                for e in range(KD):
                    wait(act, xnT_ps, s.count(KD, e + 1))
                    act.copy(xnT[:, e, :], wk[e][:, :]).then_inc(xnT_ready, 1)

            def bias_queries(s):
                wait(act, wq_loaded, 16 * WQ_LOADS)
                for m in range(KD):
                    wait(act, q_ps, s.count(KD, m + 1))
                    act.activation(qT[s.parity][:, m, :], wk[m][:, :], ACT.Identity,
                                   bias=bq_sb[:, m:m + 1]).then_inc(q_ready, 1)

            def exponentials(s, j):
                wait(act, shifted, s.count(TPG, j + 1))
                act.activation(probs[j % 2][:, 0:H * SK], probs[j % 2][:, 0:H * SK], ACT.Exp).then_inc(probs_ready, 1)

            def copy_probsT(s, j, rounds=range(3)):
                for r in rounds:
                    c0, n = ROUNDS[r]
                    wait(act, probsT_ps, s.count(3 * TPG, 3 * j + r + 1))
                    act.copy(probsT[s.parity][:, c0:c0 + n, j * P:(j + 1) * P],
                             pt[r % 2][:, 0:n * P].rearrange("p (c q) -> p c q", c=n)).then_inc(probsT_ready, 1)

            def copy_attn(s, m):
                wait(act, attn_ps, s.count(KD, m + 1))
                wait(act, attnT_ready, s.count(KD, m - 1))
                act.copy(attnU[:, m, :], wk[0][:, :]).then_inc(attnU_ready, 1)

            def place_values(s):
                if isinstance(s.pair, int):
                    src = vblk[:, s.pair, :, :]
                else:
                    src = vblk[:, bass.ds(s.pair, 1), :, :].rearrange("p b c n -> p (b c) n")
                wait(act, v_placed, 16 * V_PARTS)
                wait(act, attn_ps, s.count(KD))
                act.copy(v_now[:, :, :], src).then_inc(v_now_ready, 1)

            def copy_tT(s):
                for k in range(KD):
                    wait(act, tT_ps, s.count(KD, k + 1))
                    act.copy(tT[:, k, :], wk[k][:, :]).then_inc(tT_ready, 1)

            def step(nxt, cur, prev, old):
                if prev:
                    copy_probsT(prev, TPG - 1)
                if prev:
                    copy_attn(prev, 0)
                if cur:
                    exponentials(cur, 0)
                if old:
                    copy_tT(old)
                if cur:
                    copy_probsT(cur, 0)
                if old:
                    wait(act, lgT_ps, old.count(1, 1))
                    act.copy(lgT[:, :], wk[1][:, :]).then_inc(lgT_ready, 1)
                if cur:
                    exponentials(cur, 1)
                if prev:
                    copy_attn(prev, 1)
                if old:
                    wait(act, lsh_ready, old.count(1, 1))
                    act.activation(lexp[:, :, :], lsh[:, :, :], ACT.Exp).then_inc(lexp_ready, 1)
                if cur:
                    copy_probsT(cur, 1)
                    exponentials(cur, 2)
                    copy_probsT(cur, 2, (0, 1))
                if nxt:
                    copy_xnT(nxt)
                if cur:
                    copy_probsT(cur, 2, (2,))
                if cur and cur.parity == 0:
                    place_values(cur)
                if cur:
                    exponentials(cur, 3)
                if nxt:
                    bias_queries(nxt)

            pipeline(act, step)

            def copy_tT_slots(e):
                wait(act, tT_slots_ps, e.count(3, 1))
                act.copy(tT_slots[:, 0, 0:4 * P], pt[0][:, :]).then_inc(tT_slots_ready, 1)
                wait(act, tT_slots_ps, e.count(3, 2))
                act.copy(tT_slots[:, 1, 0:4 * P], pt[1][:, :]).then_inc(tT_slots_ready, 1)
                wait(act, tT_slots_ps, e.count(3, 3))
                act.copy(tT_slots[:, :, 4 * P:5 * P],
                         pt[0][:, 0:KD * P].rearrange("p (k s) -> p k s", k=KD)).then_inc(tT_slots_ready, 1)

            copy_tT_slots(Stage(0, 0))

            act.wait_ge(tiles_ready, 1)

            def rectify_hidden(e, following):
                def rectify(tiles):
                    n, windows = windows_of(tiles)
                    for f in range(0, FC, 3 - windows):
                        part = windows * f
                        wait(act, hidden_ps, e.count(2 * FC, 2 // windows * (part + 1)))
                        act.activation(hidden[:, f, 0:n], sc_ps[:, part % 4, 0:n],
                                       ACT.Relu).then_inc(hidden_ready[0], 3 - windows)

                by_tiles(act, e, rectify)
                if following:
                    copy_tT_slots(following)

            experts(act, rectify_hidden)

        @block.vector
        def _(dve):
            def scale_keys():
                for m in range(KD):
                    dve.wait_ge(kT_ps, m + 1)
                    dve.tensor_scalar(kT[:, m, :], wk[m][:, 0:B * SK], bk_sb[:, m:m + 1], float(DH) ** -0.5,
                                      ALU.add, ALU.mult).then_inc(kT_ready, 1)

            def prepare_mask():
                dve.wait_ge(v_loaded, 16 * V_LOADS)
                dve.tensor_scalar(mask_add[:, :, :], mask_u8[:, :].rearrange("p (b k) -> p b k", b=B),
                                  MASKED, None, ALU.mult).then_inc(mask_ready, 1)
                dve.wait_ge(consts_set, 2)
                dve.tensor_scalar(mask_row[0:1, :, :].rearrange("p b (h k) -> p b h k", h=HQ),
                                  mask_u8[0:1, :].rearrange("p (b k) -> p b k", b=B)[:, :, None, :].broadcast_to([1, B, HQ, SK]),
                                  MASKED, None, ALU.mult).then_inc(mask_ready, 1)
                dve.wait_ge(mask_ready, 2)

            def bias_values():
                for i in range(B // 2):
                    dve.wait_ge(v_ps, i + 1)
                    dve.tensor_tensor(v_nat[:, 2 * i:2 * i + 2, :], pt[i][0:SK, :].rearrange("p (b n) -> p b n", b=2),
                                      bv_sb[0:SK, None, :].broadcast_to([SK, 2, D]), ALU.add).then_inc(v_nat_ready, 1)

            def first_moments(s):
                wait(dve, x_loaded[s.parity], s.turns(16, 16))
                wait(dve, moments1, s.count(1))
                for j in range(TPG):
                    last = dve.bn_stats(bn1[:, j, :], x_sb[:, group(s, j, 1), :].rearrange("p a d -> p (a d)"))
                last.then_inc(bn1_done, 1)
                wait_alone(dve, bn1_done, s.count(1, 1))
                for j in range(TPG):
                    last = dve.bn_aggr(mv1[:, j, :], bn1[:, j, :])
                last.then_inc(moments1, 1)

            def first_norm(s):
                wait(dve, rstd1_ready, s.count(1, 1))
                wait(dve, xnT_ps, s.count(KD))
                for j in range(TPG):
                    last = dve.tensor_scalar(xn[:, j:j + 1, :], x_sb[:, group(s, j, 1), :], mv1[:, j, 0:1], rstd1[:, j:j + 1],
                                             ALU.subtract, ALU.mult)
                last.then_inc(xn_ready, 1)

            def mask_scores(s, j):
                if j in PE_MASKED:
                    return
                if isinstance(s.pair, int):
                    add = mask_add[:, s.pair, :]
                else:
                    add = mask_add[:, bass.ds(s.pair, 1), :].rearrange("p b k -> p (b k)")
                wait(dve, scores_ready, s.count(TPG, j + 1))
                wait(dve, probsT_ps, s.count(3 * TPG, 3 * (j - 1)))
                wait(dve, sums_ready, s.count(TPG, j - 1))
                dve.tensor_tensor(by_head(j), scores, add[:, None, None, :].broadcast_to([P, 4, HQ, SK]),
                                  ALU.add).then_inc(scores_read, 1)
                wait(dve, scores_read, s.count(TPG, j + 1))

            def by_head(j):
                return probs[j % 2][:, 0:H * SK].rearrange("p (q h k) -> p q h k", q=4, h=HQ)

            def shift_scores(s, j):
                m = rowmax[:, j % 2, :]
                if j in PE_MASKED:
                    src = scores
                    wait(dve, scores_ready, s.count(TPG, j + 1))
                    wait(dve, probsT_ps, s.count(3 * TPG, 3 * (j - 1)))
                    wait(dve, sums_ready, s.count(TPG, j - 1))
                else:
                    src = by_head(j)
                dve.tensor_reduce(m, src, AX.X, ALU.max).then_inc(rowmax_ready, 1)
                wait(dve, rowmax_ready, s.count(TPG, j + 1))
                dve.tensor_tensor(by_head(j), src, m.rearrange("p (q h) -> p q h", q=4)[:, :, :, None].broadcast_to([P, 4, HQ, SK]),
                                  ALU.subtract).then_inc(shifted, 1)
                if j in PE_MASKED:
                    wait(dve, shifted, s.count(TPG, j + 1))
                    dve.sem_inc(scores_read, 1)

            def sum_probs(s, j):
                wait(dve, probs_ready, s.count(TPG, j + 1))
                if j == 0:
                    wait(dve, rsum_ready, s.count(1))
                dve.tensor_reduce(sums[:, j, :], probs[j % 2][:, 0:H * SK].rearrange("p (h k) -> p h k", h=H),
                                  AX.X, ALU.add).then_inc(sums_ready, 1)

            def invert_sums(s):
                wait(dve, sums_ready, s.count(TPG, TPG))
                wait(dve, rsum_wide_ready, s.count(1))
                dve.reciprocal(rsum[:, :, :], sums[:, :, :]).then_inc(rsum_ready, 1)

            def normalise_attn(s, m):
                wait(dve, attnU_ready, s.count(KD, m + 1))
                wait(dve, rsumT_ps, s.count(KD, m + 1))
                wait(dve, proj_ps, s.count(2))
                dve.tensor_tensor(attnT[:, m, :], attnU[:, m, :], pt[1 - m][:, :], ALU.mult).then_inc(attnT_ready, 1)

            def add_residual(s):
                r = rows[s.parity]
                wait(dve, xb_ready, s.count(1, 1))
                wait(dve, rows_free, s.count(1, 1))
                wait(dve, base_ready, s.count(1))
                for h in range(2):
                    wait(dve, proj_ps, s.count(2, h + 1))
                    dve.tensor_tensor(r[:, 2 * h:2 * h + 2, 0:D], wk[h][:, :].rearrange("p (t d) -> p t d", t=2),
                                      x_sb[:, group(s, 2 * h, 2), :], ALU.add).then_inc(x1_ready, 1)

            def second_moments(s):
                r = rows[s.parity]
                wait(dve, x1_ready, s.count(2, 2))
                wait(dve, t_ready, s.count(1))
                for j in range(TPG):
                    last = dve.bn_stats(bn2[:, j, :], r[:, j, 0:D])
                last.then_inc(bn2_done, 1)
                wait_alone(dve, bn2_done, s.count(1, 1))
                for j in range(TPG):
                    last = dve.bn_aggr(mv2[:, j, :], bn2[:, j, :])
                last.then_inc(moments2, 1)

            def second_norm(s):
                r = rows[s.parity]
                wait(dve, rstd2_step, s.count(8, 8))
                wait(dve, tT_ps, s.count(KD))
                for j in range(TPG):
                    last = dve.tensor_scalar(t_sb[:, j, :], r[:, j, 0:D], r[:, j, MEAN:MEAN + 1], r[:, j, RSTD:RSTD + 1],
                                             ALU.subtract, ALU.mult)
                last.then_inc(t_ready, 1)

            def choose(s):
                def then(k, ins):
                    ins.then_inc(choice_step, 1)
                    dve.wait_ge(choice_step, s.count(3, k))
                logits = wk[1][:, :].rearrange("p (t c) -> p t c", t=TPG)[:, :, 0:E]
                wait(dve, logits_ps, s.count(1, 1))
                then(1, dve.tensor_reduce(lmax[:, :], logits, AX.X, ALU.max))
                dve.tensor_tensor(lsh[:, :, :], logits, lmax[:, :, None].broadcast_to([P, TPG, E]),
                                  ALU.subtract).then_inc(lsh_ready, 1)
                dve.wait_ge(lsh_ready, s.count(1, 1))
                then(2, dve.scalar_tensor_tensor(cand[:, :, :], lsh[:, :, :], 0.0, rank[:, :, :], ALU.is_equal, ALU.mult))
                then(3, dve.tensor_reduce(cmax[:, :], cand[:, :, :], AX.X, ALU.max))
                dve.tensor_tensor(onehot[:, :, :], cand[:, :, :], cmax[:, :, None].broadcast_to([P, TPG, E]),
                                  ALU.is_equal).then_inc(onehot_ready, 1)

            def place(s):
                def then(k, ins):
                    ins.then_inc(place_step, 1)
                    dve.wait_ge(place_step, s.count(3, k))
                r = rows[s.parity]
                wait(dve, prefix_ps, s.count(1, 1))
                dve.tensor_tensor(posm[:, :, :], wk[1][:, 0:TPG * E].rearrange("p (t e) -> p t e", t=TPG),
                                  onehot[:, :, :], ALU.mult).then_inc(posm_ready, 1)
                dve.tensor_reduce(group_taken[:, :], onehot[:, :, :].rearrange("p t e -> p e t"), AX.X, ALU.add)
                wait(dve, lexp_ready, s.count(1, 1))
                dve.tensor_reduce(esum[:, :], lexp[:, :, :], AX.X, ALU.add)
                wait(dve, scales_ready, s.count(1, 1))
                then(1, dve.tensor_scalar(first[:, :], cmax[:, :], float(-CAP), float(E * CAP), ALU.mult, ALU.add))
                dve.tensor_tensor(taken[:, :], taken[:, :], group_taken[:, :], ALU.add).then_inc(taken_ready, 1)
                dve.reciprocal(pmax[:, :], esum[:, :])
                then(2, dve.tensor_reduce(pos[:, :], posm[:, :, :], AX.X, ALU.add))
                dve.tensor_scalar(keep[:, :], pos[:, :], float(CAP), None, ALU.is_lt)
                dve.tensor_scalar(past[:, :], pos[:, :], float(CAP), FAR, ALU.is_ge, ALU.mult)
                then(3, dve.tensor_tensor(slotf[:, :], first[:, :], pos[:, :], ALU.add))
                dve.tensor_tensor(slot[s.parity][:, :], slotf[:, :], past[:, :], ALU.add)
                dve.tensor_tensor(r[:, :, GATE], pmax[:, :], keep[:, :], ALU.mult)
                dve.tensor_copy(r[:, :, TOKEN], token_no[:, group(s)]).then_inc(route_ready, 1)

            def step(nxt, cur, prev, old):
                if cur:
                    mask_scores(cur, 0)
                    shift_scores(cur, 0)
                if prev:
                    sum_probs(prev, TPG - 1)
                    invert_sums(prev)
                if cur:
                    mask_scores(cur, 1)
                    shift_scores(cur, 1)
                if nxt:
                    first_moments(nxt)
                if cur is None and nxt:
                    scale_keys()
                if cur:
                    sum_probs(cur, 0)
                if old:
                    choose(old)
                if prev:
                    normalise_attn(prev, 0)
                    normalise_attn(prev, 1)
                if nxt:
                    first_norm(nxt)
                if cur is None and nxt:
                    prepare_mask()
                    bias_values()
                if cur:
                    mask_scores(cur, 2)
                if old:
                    place(old)
                if cur:
                    shift_scores(cur, 2)
                    sum_probs(cur, 1)
                if prev:
                    add_residual(prev)
                if cur:
                    mask_scores(cur, 3)
                    shift_scores(cur, 3)
                if prev:
                    second_moments(prev)
                if cur:
                    sum_probs(cur, 2)
                if prev:
                    second_norm(prev)

            pipeline(dve, step)

            def normalise_slots(e):
                r = srow[e.parity]
                wait(dve, srow_loaded[e.parity], e.turns(16, 16))
                wait(dve, tT_slots_ps, e.count(3))
                for c in range(SC):
                    last = dve.tensor_scalar(t_slots[:, c, :], r[:, c, 0:D], r[:, c, MEAN:MEAN + 1], r[:, c, RSTD:RSTD + 1],
                                             ALU.subtract, ALU.mult)
                last.then_inc(t_slots_ready, 1)

            def destinations(e):
                r = srow[e.parity]
                wait(dve, y_sent[e.parity], e.turns(16 * SC))
                wait(dve, dest_ready, e.count(1))
                dve.tensor_scalar(empty[:, :], r[:, :, TOKEN], 0.0, FAR, ALU.is_equal, ALU.mult).then_inc(empty_ready, 1)
                dve.wait_ge(empty_ready, e.count(1, 1))
                dve.scalar_tensor_tensor(dest[e.parity][:, :], r[:, :, TOKEN], -1.0, empty[:, :],
                                         ALU.add, ALU.add).then_inc(dest_ready, 1)

            dve.wait_ge(totals_ps, 1)
            tiles_before = None
            for i, full in enumerate(range(MIN_TILES, SC)):
                result = tiles_used if full == SC - 1 else tiles_f[i % 2]
                if i == 0:
                    last = dve.tensor_scalar(result[:, :], wk[0][:, 0:E], float(full * P), float(MIN_TILES), ALU.is_gt, ALU.add)
                else:
                    dve.wait_ge(tiles_step, i)
                    last = dve.scalar_tensor_tensor(result[:, :], wk[0][:, 0:E], float(full * P), tiles_before[:, :],
                                                    ALU.is_gt, ALU.add)
                last.then_inc(tiles_ready if full == SC - 1 else tiles_step, 1)
                tiles_before = result
            dve.wait_ge(tiles_ready, 1)
            normalise_slots(Stage(0, 0))

            def expert_step(e, following):
                def rectify_and_weigh(tiles):
                    n, windows = windows_of(tiles)
                    for f in range(2 - windows, FC, 3 - windows):
                        if following and f == FC // 2 + 2 - windows:
                            normalise_slots(following)
                        part = windows * f + windows - 1
                        wait(dve, hidden_ps, e.count(2 * FC, 2 // windows * (part + 1)))
                        dve.tensor_scalar(hidden[:, f, (windows - 1) * n:windows * n], sc_ps[:, part % 4, 0:n],
                                          0.0, None, ALU.max).then_inc(hidden_ready[1], 3 - windows)
                    destinations(e)
                    for c in range(tiles):
                        wait(dve, y_ps, e.count(SC, c + 1))
                        dve.scalar_tensor_tensor(y_sb[e.parity][:, c, :], wk[(SC * e.parity + c) % 2][:, 0:D],
                                                 srow[e.parity][:, c, GATE:GATE + 1], srow[e.parity][:, c, 0:D],
                                                 ALU.mult, ALU.add).then_inc(y_ready, skipped_too(c, tiles))

                by_tiles(dve, e, rectify_and_weigh)

            experts(dve, expert_step)

        @block.tensor
        def _(pe):
            pe.wait_ge(k_loaded, 16 * K_LOADS)
            for m in range(KD):
                for k in range(KD):
                    last = pe.matmul(wk[m][:, 0:B * SK], wk_sb[:, k, m * P:(m + 1) * P], ctx_sb[:, k, :],
                                     start=(k == 0), stop=(k == KD - 1))
                last.then_inc(kT_ps, 1)
            pe.wait_ge(consts_cut, 2)
            pe.wait_ge(kT_ready, KD)

            def values(first):
                pe.wait_ge(v_loaded, 16 * V_LOADS)
                for b in range(first, first + 2):
                    for k in range(KD):
                        last = pe.matmul(pt[b // 2][0:SK, (b % 2) * D:(b % 2 + 1) * D], ctx_sb[:, k, b * SK:(b + 1) * SK],
                                         wv_sb[:, k, :], start=(k == 0), stop=(k == KD - 1))
                    if b % 2:
                        last.then_inc(v_ps, 1)

            def transpose_xn(s):
                wait(pe, xn_ready, s.count(1, 1))
                wait(pe, x1_ready, s.count(2, -2))
                wait(pe, q_ready, s.count(KD))
                for k in range(KD):
                    for j in range(TPG):
                        last = pe.transpose(wk[k][:, j * P:(j + 1) * P], xn[:, j, k * P:(k + 1) * P], ident[:, :])
                    last.then_inc(xnT_ps, 1)

            def queries(s):
                wait(pe, wq_loaded, 16 * WQ_LOADS)
                wait(pe, xnT_ready, s.count(KD, KD))
                for m in range(KD):
                    for k in range(KD):
                        last = pe.matmul(wk[m][:, :], wq_sb[:, k, m * P:(m + 1) * P], xnT[:, k, :],
                                         start=(k == 0), stop=(k == KD - 1))
                    last.then_inc(q_ps, 1)

            def score(s, j):
                if j == 0:
                    wait(pe, q_ready, s.count(KD, KD))
                if isinstance(s.pair, int):
                    mrow, krow = mask_row[:, s.pair, :], kflat[:, s.pair, :, :]
                else:
                    mrow = mask_row[:, bass.ds(s.pair, 1), :].rearrange("p b c -> p (b c)")
                    krow = kflat[:, bass.ds(s.pair, 1), :, :].rearrange("p b m c -> p (b m) c")
                wait(pe, scores_read, s.count(TPG, j))
                if j == PE_MASKED[0]:
                    wait(pe, mask_ready, 2)
                for q in range(4):
                    m, c = q // 2, (q % 2) * HQ * SK
                    if j in PE_MASKED:
                        pe.matmul(sc_ps[:, q, 0:HQ * SK], ones[:, :], mrow, start=True, stop=False)
                    last = pe.matmul(sc_ps[:, q, 0:HQ * SK], qT[s.parity][:, m, j * P:(j + 1) * P],
                                     krow[:, m, c:c + HQ * SK], start=j not in PE_MASKED, stop=True)
                last.then_inc(scores_ready, 1)

            def transpose_probs(s, j, rounds=range(3)):
                wait(pe, probs_ready, s.count(TPG, j + 1))
                if j == 1 and 0 in rounds:
                    wait(pe, attnT_ready, s.count(KD))
                for r in rounds:
                    c0, n = ROUNDS[r]
                    wait(pe, probsT_ready, s.count(3 * TPG, 3 * j + (1 if r == 2 else 0)))
                    for i in range(n):
                        m, c = (c0 + i) // CH, (c0 + i) % CH
                        at = m * HH * SK + c * P
                        last = pe.transpose(pt[r % 2][:, i * P:(i + 1) * P], probs[j % 2][:, at:at + P], ident[:, :])
                    last.then_inc(probsT_ps, 1)

            def transpose_rsum(s, running):
                wait(pe, rsum_wide_ready, s.count(1, 1))
                wait(pe, probsT_ready, s.count(3 * TPG, 3 * TPG + (3 if running else 0)))
                for m in range(KD):
                    for j in range(TPG):
                        last = pe.transpose(pt[1 - m][:, j * P:(j + 1) * P], rsum_wide[:, j, m * P:(m + 1) * P], ident[:, :])
                    last.then_inc(rsumT_ps, 1)

            def weigh_values(s, m, ahead):
                if m == 0:
                    wait(pe, probsT_ready, s.count(3 * TPG, 3 * TPG))
                    wait(pe, v_now_ready, s.turns(1, 1))
                    wait(pe, x1_ready, s.count(2))
                    wait(pe, q_ready, s.count(KD, 2 * KD if ahead else KD))
                else:
                    wait(pe, tT_ready, s.count(KD))
                    wait(pe, attnU_ready, s.count(KD, 1))
                for c in range(CH):
                    last = pe.matmul(wk[0][:, :], v_now[:, m * CH + c, :], probsT[s.parity][:, m * CH + c, :],
                                     start=(c == 0), stop=(c == CH - 1))
                last.then_inc(attn_ps, 1)

            def project(s, halves=range(2)):
                wait(pe, attnT_ready, s.count(KD, KD))
                for h in halves:
                    if h == 1:
                        wait(pe, posm_ready, s.count(1))
                    for j in range(2):
                        for m in range(KD):
                            last = pe.matmul(wk[h][:, j * D:(j + 1) * D], attnT[:, m, (2 * h + j) * P:(2 * h + j + 1) * P],
                                             wo_sb[:, m, :], start=(m == 0), stop=(m == KD - 1))
                    last.then_inc(proj_ps, 1)

            def transpose_t(s, following):
                wait(pe, t_ready, s.count(1, 1))
                if following:
                    wait(pe, attnU_ready, s.count(KD, KD + 1))
                for k in range(KD):
                    for j in range(TPG):
                        last = pe.transpose(wk[k][:, j * P:(j + 1) * P], t_sb[:, j, k * P:(k + 1) * P], ident[:, :])
                    last.then_inc(tT_ps, 1)

            def router_logits(s):
                wait(pe, tT_ready, s.count(KD, KD))
                for k in range(KD):
                    last = pe.matmul(wk[1][:, :], wr_sb[:, k, :], tT[:, k, :], start=(k == 0), stop=(k == KD - 1))
                last.then_inc(lgT_ps, 1)

            def transpose_logits(s):
                wait(pe, lgT_ready, s.count(1, 1))
                for j in range(TPG):
                    last = pe.transpose(wk[1][:, j * P:(j + 1) * P], lgT[:, j * P:(j + 1) * P], ident[:, :])
                last.then_inc(logits_ps, 1)

            def count_before(s):
                wait(pe, onehot_ready, s.count(1, 1))
                wait(pe, taken_ready, s.count(1, 1))
                dst = wk[1][:, 0:TPG * E]
                pe.matmul(dst, before[:, :], onehot[:, :, :], start=True, stop=False)
                for j in range(TPG):
                    pe.matmul(wk[1][:, j * E:(j + 1) * E], ones[:, :], taken[:, :], start=False, stop=False)
                for j in range(1, TPG):
                    for i in range(j):
                        last = pe.matmul(wk[1][:, j * E:(j + 1) * E], ones[:, :], onehot[:, i, :], start=False,
                                         stop=(j == TPG - 1 and i == j - 1))
                last.then_inc(prefix_ps, 1)

            def step(nxt, cur, prev, old):
                if prev:
                    transpose_probs(prev, TPG - 1)
                if cur:
                    if cur.parity == 0:
                        wait(pe, kblk_ready, cur.turns(KD, KD))
                    score(cur, 0)
                if prev:
                    weigh_values(prev, 0, cur is not None)
                if cur:
                    score(cur, 1)
                if cur and prev is None:
                    pe.wait_ge(v_nat_ready, B // 2)
                    pe.wait_ge(w_attn_loaded, 16 * ATTN_W_LOADS)
                if old:
                    transpose_t(old, prev is not None)
                if cur:
                    transpose_probs(cur, 0, (0, 1))
                if old:
                    router_logits(old)
                if cur:
                    transpose_probs(cur, 0, (2,))
                if prev:
                    weigh_values(prev, 1, None)
                if old:
                    transpose_logits(old)
                if prev:
                    transpose_rsum(prev, cur is not None)
                if cur:
                    score(cur, 2)
                if old:
                    count_before(old)
                if cur:
                    transpose_probs(cur, 1)
                if prev:
                    project(prev)
                if cur:
                    score(cur, 3)
                    transpose_probs(cur, 2, (0, 1))
                if nxt:
                    transpose_xn(nxt)
                if cur is None and nxt:
                    values(0)
                if cur:
                    transpose_probs(cur, 2, (2,))
                if nxt:
                    queries(nxt)
                if cur is None and nxt:
                    values(2)

            pipeline(pe, step)

            def transpose_slots(e):
                wait(pe, t_slots_ready, e.count(1, 1))
                wait(pe, tT_slots_ready, e.count(3))
                for k in range(KD):
                    for c in range(4):
                        last = pe.transpose(pt[k][:, c * P:(c + 1) * P], t_slots[:, c, k * P:(k + 1) * P], ident[:, :])
                    last.then_inc(tT_slots_ps, 1)

            def transpose_last_slots(e):
                wait(pe, tT_slots_ready, e.count(3, 1))
                for k in range(KD):
                    last = pe.transpose(pt[0][:, k * P:(k + 1) * P], t_slots[:, 4, k * P:(k + 1) * P], ident[:, :])
                last.then_inc(tT_slots_ps, 1)

            pe.wait_ge(taken_ready, NG + 1)
            pe.wait_ge(x1_ready, 2 * NG)
            pe.matmul(wk[0][:, 0:E], ones[:, :], taken[:, :], start=True, stop=True).then_inc(totals_ps, 1)
            transpose_slots(Stage(0, 0))
            transpose_last_slots(Stage(0, 0))
            pe.wait_ge(tiles_ready, 1)

            def expert_step(e, following):
                def products(tiles):
                    n, windows = windows_of(tiles)
                    for f in range(FC):
                        for w in range(windows):
                            part = windows * f + w
                            if part >= 4:
                                wait(pe, hidden_ready[part % 2], e.count(FC, (3 - windows) * ((part - 4) // 2 + 1)))
                            for k in range(KD):
                                last = pe.matmul(sc_ps[:, part % 4, 0:n], w1_sb[e.parity][:, k, f * P:(f + 1) * P],
                                                 tT_slots[:, k, w * n:(w + 1) * n], start=(k == 0), stop=(k == KD - 1))
                            last.then_inc(hidden_ps, 2 // windows)
                    if following:
                        transpose_slots(following)
                    for half in range(2):
                        wait(pe, hidden_ready[half], e.count(FC, FC))
                    for c in range(tiles):
                        wait(pe, y_ready, e.count(SC, c - 1))
                        for f in range(FC):
                            last = pe.matmul(wk[(SC * e.parity + c) % 2][:, 0:D], hidden[:, f, c * P:(c + 1) * P],
                                             w2_sb[e.parity][:, f, :], start=(f == 0), stop=(f == FC - 1))
                        last.then_inc(y_ps, skipped_too(c, tiles))
                        if following and c == 0:
                            transpose_last_slots(following)

                wait(pe, w_loaded[e.parity], e.turns(32, 32))
                wait(pe, tT_slots_ready, e.count(3, 3))
                by_tiles(pe, e, products)

            experts(pe, expert_step)


def kernel(x, ctx_1024, mask_BxS2_bk0, L0_xattn_Wq, L0_xattn_bq, L0_xattn_Wk, L0_xattn_bk, L0_xattn_Wv, L0_xattn_bv,
           L0_xattn_Wo, L0_xattn_bo, L0_ffn_Wr, L0_ffn_W1, L0_ffn_W2):
    import concourse.bacc as bacc
    from concourse.bass_utils import run_bass_kernel_spmd

    arrays = {
        "in_x": np.asarray(x),
        "in_ctxT": np.asarray(ctx_1024).reshape(B * SK, D).T,
        "in_mask": np.asarray(mask_BxS2_bk0),
        "in_wqT": np.asarray(L0_xattn_Wq).T, "in_bq": np.asarray(L0_xattn_bq).reshape(KD, P).T,
        "in_wkT": np.asarray(L0_xattn_Wk).T, "in_bk": np.asarray(L0_xattn_bk).reshape(KD, P).T,
        "in_wvT": np.asarray(L0_xattn_Wv).T, "in_bv": np.asarray(L0_xattn_bv),
        "in_woT": np.asarray(L0_xattn_Wo).T, "in_bo": np.asarray(L0_xattn_bo),
        "in_wr": np.asarray(L0_ffn_Wr), "in_w1": np.asarray(L0_ffn_W1), "in_w2": np.asarray(L0_ffn_W2),
    }
    arrays = {name: np.ascontiguousarray(a) for name, a in arrays.items()}
    nc = bacc.Bacc("TRN2", target_bir_lowering=False, num_devices=1)
    args = [nc.dram_tensor(name, a.shape, mybir.dt.from_np(a.dtype), kind="ExternalInput").ap() for name, a in arrays.items()]
    args.append(nc.dram_tensor("out_x", (B, S, D), F32, kind="ExternalOutput").ap())
    xattn_moe(nc, *args)
    r = run_bass_kernel_spmd(nc, [arrays], core_ids=[0])
    return r.results[0]["out_x"]
```
